# Optimizing a Trainium2 kernel written in Bass

```python
import numpy as np
import jax
import jax.numpy as jnp

def _softmax(x, axis=-1):
    return jax.nn.softmax(x, axis=axis)

def _gelu(x):
    return jax.nn.gelu(x, approximate=True)

def _silu(x):
    return jax.nn.silu(x)

def _sigmoid(x):
    return jax.nn.sigmoid(x)

def _layernorm(x, axis=-1, eps=1e-05):
    m = jnp.mean(x, axis=axis, keepdims=True)
    v = jnp.var(x, axis=axis, keepdims=True)
    return (x - m) / jnp.sqrt(v + eps)

def _scatter_add(tgt, idx, src, axis=0):
    return tgt.at[idx].add(src)

def _segment_sum(src, seg, n):
    return jax.ops.segment_sum(src, seg, n)
kernel_name = 'mk_xattn_seq_d2_seqx_r8_39a634'

def setup_inputs(seed: int=0):
    np.random.seed(seed)
    _w = jnp.asarray

    def _rec_inputs():
        import jax
        import jax.numpy as jnp
        _rk = jax.random.key(seed)
        x = 7.22e-05 + 1 * jax.random.normal(jax.random.fold_in(_rk, 1), (16, 64, 256), jnp.float32)
        _lenS = 64 - jax.random.randint(jax.random.fold_in(_rk, 7), (16,), 0, max(1, 64 // 4) + 1, jnp.int32)
        _lenS2 = 64 - jax.random.randint(jax.random.fold_in(_rk, 8), (16,), 0, max(1, 64 // 4) + 1, jnp.int32)
        _ctx_2048P = jax.random.normal(jax.random.fold_in(_rk, 11), (16, 16, 256), jnp.float32)
        _ctx_2048c = jax.random.dirichlet(jax.random.fold_in(_rk, 511), 0.3 * jnp.ones((16,), jnp.float32), (16, 64))
        _ctx_2048t = jnp.einsum('bsk,bkd->bsd', _ctx_2048c, _ctx_2048P)
        _ctx_2048t = _ctx_2048t * jax.lax.rsqrt(jnp.mean(jnp.square(_ctx_2048t)) + 1e-12) * 0.953939
        ctx_2048 = 4.13588e-05 + 0.999923 * (_ctx_2048t + 0.3 * jax.random.normal(jax.random.fold_in(_rk, 611), (16, 64, 256), jnp.float32))
        _validS = jnp.arange(64)[None, :] < _lenS[:, None]
        _validS2 = jnp.arange(64)[None, :] < _lenS2[:, None]
        _causal = jnp.tril(jnp.ones((64, 64), dtype=bool))
        mask_BxS2_bf1 = jnp.ones((16, 64), dtype=bool)
        return (x, ctx_2048, mask_BxS2_bf1)
    x, ctx_2048, mask_BxS2_bf1 = _rec_inputs()

    def _L0_xattn_setup():
        import jax, jax.numpy as jnp
        import numpy as np
        B, C, N = (8, 64, 256)
        key = jax.random.key(seed)
        ks = jax.random.split(key, 7)
        s = 1.0 / np.sqrt(C)
        return {'x': jax.random.normal(ks[0], (B, C, N), dtype=jnp.float32), 'y': jax.random.normal(ks[1], (B, C, N), dtype=jnp.float32), 'w_qk': jax.random.normal(ks[2], (C, C), dtype=jnp.float32) * s, 'w_v': jax.random.normal(ks[3], (C, C), dtype=jnp.float32) * s, 'b_v': jax.random.normal(ks[4], (C,), dtype=jnp.float32) * s, 'w_t': jax.random.normal(ks[5], (C, C), dtype=jnp.float32) * s, 'b_t': jax.random.normal(ks[6], (C,), dtype=jnp.float32) * s}
    _L0_xattn_all = _L0_xattn_setup()
    _L0_xattn_in = {k: v for k, v in _L0_xattn_all.items() if k in ('w_qk', 'w_v', 'b_v', 'w_t', 'b_t')}
    del _L0_xattn_all

    def _L1_xattn_setup():
        import jax, jax.numpy as jnp
        import numpy as np
        D = 256
        H = 16
        HD = D // H
        INNER = 4 * D
        EPS = 1e-05

        def layer_norm(x, w, b):
            mu = jnp.mean(x, axis=-1, keepdims=True)
            var = jnp.mean(jnp.square(x - mu), axis=-1, keepdims=True)
            return (x - mu) * jax.lax.rsqrt(var + EPS) * w + b
        key = jax.random.key(seed)
        ks = jax.random.split(key, 12)
        B, LQ, LK = (4, 128, 256)
        std = 0.02
        inp = {'hidden_states': jax.random.normal(ks[0], (B, LQ, D), jnp.float32), 'encoder_hidden_states': jax.random.normal(ks[1], (B, LK, D), jnp.float32), 'encoder_attention_mask': jnp.ones((B, LK), dtype=bool), 'ln1_w': jnp.ones((D,), jnp.float32), 'ln1_b': jnp.zeros((D,), jnp.float32), 'q_w': jax.random.normal(ks[2], (D, D), jnp.float32) * std, 'q_b': jnp.zeros((D,), jnp.float32), 'k_w': jax.random.normal(ks[3], (D, D), jnp.float32) * std, 'k_b': jnp.zeros((D,), jnp.float32), 'v_w': jax.random.normal(ks[4], (D, D), jnp.float32) * std, 'v_b': jnp.zeros((D,), jnp.float32), 'cproj_w': jax.random.normal(ks[5], (D, D), jnp.float32) * std, 'cproj_b': jnp.zeros((D,), jnp.float32), 'ln2_w': jnp.ones((D,), jnp.float32), 'ln2_b': jnp.zeros((D,), jnp.float32), 'fc_w': jax.random.normal(ks[6], (D, INNER), jnp.float32) * std, 'fc_b': jnp.zeros((INNER,), jnp.float32), 'proj_w': jax.random.normal(ks[7], (INNER, D), jnp.float32) * std, 'proj_b': jnp.zeros((D,), jnp.float32)}
        return inp
    _L1_xattn_all = _L1_xattn_setup()
    _L1_xattn_in = {k: v for k, v in _L1_xattn_all.items() if k in ('ln1_w', 'ln1_b', 'q_w', 'q_b', 'k_w', 'k_b', 'v_w', 'v_b', 'cproj_w', 'cproj_b', 'ln2_w', 'ln2_b', 'fc_w', 'fc_b', 'proj_w', 'proj_b')}
    del _L1_xattn_all
    return {'x': x, 'ctx_2048': ctx_2048, 'mask_BxS2_bf1': mask_BxS2_bf1, 'L0_xattn_w_qk': _L0_xattn_in['w_qk'], 'L0_xattn_w_v': _L0_xattn_in['w_v'], 'L0_xattn_b_v': _L0_xattn_in['b_v'], 'L0_xattn_w_t': _L0_xattn_in['w_t'], 'L0_xattn_b_t': _L0_xattn_in['b_t'], 'L1_xattn_ln1_w': _L1_xattn_in['ln1_w'], 'L1_xattn_ln1_b': _L1_xattn_in['ln1_b'], 'L1_xattn_q_w': _L1_xattn_in['q_w'], 'L1_xattn_q_b': _L1_xattn_in['q_b'], 'L1_xattn_k_w': _L1_xattn_in['k_w'], 'L1_xattn_k_b': _L1_xattn_in['k_b'], 'L1_xattn_v_w': _L1_xattn_in['v_w'], 'L1_xattn_v_b': _L1_xattn_in['v_b'], 'L1_xattn_cproj_w': _L1_xattn_in['cproj_w'], 'L1_xattn_cproj_b': _L1_xattn_in['cproj_b'], 'L1_xattn_ln2_w': _L1_xattn_in['ln2_w'], 'L1_xattn_ln2_b': _L1_xattn_in['ln2_b'], 'L1_xattn_fc_w': _L1_xattn_in['fc_w'], 'L1_xattn_fc_b': _L1_xattn_in['fc_b'], 'L1_xattn_proj_w': _L1_xattn_in['proj_w'], 'L1_xattn_proj_b': _L1_xattn_in['proj_b']}

def reference(x, ctx_2048, mask_BxS2_bf1, L0_xattn_w_qk, L0_xattn_w_v, L0_xattn_b_v, L0_xattn_w_t, L0_xattn_b_t, L1_xattn_ln1_w, L1_xattn_ln1_b, L1_xattn_q_w, L1_xattn_q_b, L1_xattn_k_w, L1_xattn_k_b, L1_xattn_v_w, L1_xattn_v_b, L1_xattn_cproj_w, L1_xattn_cproj_b, L1_xattn_ln2_w, L1_xattn_ln2_b, L1_xattn_fc_w, L1_xattn_fc_b, L1_xattn_proj_w, L1_xattn_proj_b):
    import jax
    import jax.numpy as jnp

    def _L0_xattn_ref(x, y, w_qk, w_v, b_v, w_t, b_t):
        import jax, jax.numpy as jnp
        import numpy as np
        B, C, N = (8, 64, 256)
        x_q = jnp.einsum('oc,bcn->bno', w_qk, y)
        x_k = jnp.einsum('oc,bcn->bon', w_qk, x)
        x_v = jnp.einsum('oc,bcn->bon', w_v, x) + b_v[None, :, None]
        energy = jnp.einsum('bnc,bcm->bnm', x_q, x_k)
        attention = jax.nn.softmax(energy, axis=-1)
        attention = attention / (1e-07 + attention.sum(axis=1, keepdims=True))
        x_r = jnp.einsum('bcn,bnm->bcm', x_v, attention)
        x_r = jax.nn.relu(jnp.einsum('oc,bcn->bon', w_t, x - x_r) + b_t[None, :, None])
        return x + x_r

    def _L1_xattn_ref(hidden_states, encoder_hidden_states, encoder_attention_mask, ln1_w, ln1_b, q_w, q_b, k_w, k_b, v_w, v_b, cproj_w, cproj_b, ln2_w, ln2_b, fc_w, fc_b, proj_w, proj_b):
        import jax, jax.numpy as jnp
        import numpy as np
        D = 256
        H = 16
        HD = D // H
        INNER = 4 * D
        EPS = 1e-05

        def layer_norm(x, w, b):
            mu = jnp.mean(x, axis=-1, keepdims=True)
            var = jnp.mean(jnp.square(x - mu), axis=-1, keepdims=True)
            return (x - mu) * jax.lax.rsqrt(var + EPS) * w + b
        B, LQ, _ = hidden_states.shape
        LK = encoder_hidden_states.shape[1]
        residual = hidden_states
        x = layer_norm(hidden_states, ln1_w, ln1_b)
        q = (x @ q_w + q_b).reshape(B, LQ, H, HD).transpose(0, 2, 1, 3)
        k = (encoder_hidden_states @ k_w + k_b).reshape(B, LK, H, HD).transpose(0, 2, 1, 3)
        v = (encoder_hidden_states @ v_w + v_b).reshape(B, LK, H, HD).transpose(0, 2, 1, 3)
        scale = 1.0 / np.sqrt(HD).astype(np.float32)
        scores = jnp.einsum('bhqd,bhkd->bhqk', q, k) * scale
        mask = encoder_attention_mask[:, None, None, :]
        mask_value = jnp.finfo(scores.dtype).min
        scores = jnp.where(mask, scores, mask_value)
        attn = jax.nn.softmax(scores, axis=-1)
        out = jnp.einsum('bhqk,bhkd->bhqd', attn, v)
        out = out.transpose(0, 2, 1, 3).reshape(B, LQ, D)
        out = out @ cproj_w + cproj_b
        hidden = out + residual
        residual = hidden
        y = layer_norm(hidden, ln2_w, ln2_b)
        y = jax.nn.gelu(y @ fc_w + fc_b, approximate=True)
        y = y @ proj_w + proj_b
        return residual + y
    x = _L0_xattn_ref(x, ctx_2048, L0_xattn_w_qk, L0_xattn_w_v, L0_xattn_b_v, L0_xattn_w_t, L0_xattn_b_t)
    x = _L1_xattn_ref(x, ctx_2048, mask_BxS2_bf1, L1_xattn_ln1_w, L1_xattn_ln1_b, L1_xattn_q_w, L1_xattn_q_b, L1_xattn_k_w, L1_xattn_k_b, L1_xattn_v_w, L1_xattn_v_b, L1_xattn_cproj_w, L1_xattn_cproj_b, L1_xattn_ln2_w, L1_xattn_ln2_b, L1_xattn_fc_w, L1_xattn_fc_b, L1_xattn_proj_w, L1_xattn_proj_b)
    return x

_drawn_inputs = setup_inputs


def setup_inputs(seed=0):
    import zlib

    import numpy as np

    out = dict(_drawn_inputs(seed))
    spreads = {'L1_xattn_ln1_w': (1.0, 0.6),
     'L1_xattn_ln1_b': (0.0, 0.8),
     'L1_xattn_q_b': (0.0, 0.8),
     'L1_xattn_k_b': (0.0, 0.8),
     'L1_xattn_v_b': (0.0, 0.345),
     'L1_xattn_cproj_b': (0.0, 0.1),
     'L1_xattn_ln2_w': (1.0, 0.6),
     'L1_xattn_ln2_b': (0.0, 0.8),
     'L1_xattn_fc_b': (0.0, 0.282),
     'L1_xattn_proj_b': (0.0, 0.1)}
    factors = {'L1_xattn_q_w': 8.0, 'L1_xattn_k_w': 8.0}
    for name, (base, spread) in spreads.items():
        noise = np.random.default_rng([zlib.crc32(name.encode()), seed]).standard_normal(out[name].shape)
        drawn = base * np.exp(spread * noise) if base else spread * noise
        out[name] = jnp.asarray(drawn.astype(out[name].dtype))
    for name, factor in factors.items():
        out[name] = (out[name] * factor).astype(out[name].dtype)
    return out
```

```python
from contextlib import ExitStack

import concourse.bass as bass
from concourse import mybir

F32 = mybir.dt.float32
U8 = mybir.dt.uint8
ALU = mybir.AluOpType
ACT = mybir.ActivationFunctionType
AX = mybir.AxisListType

P = 128
BANK = 512
EXP_LN_SET = 6
FLOAT_MIN = -3.4028234663852886e38
LN_EPS = 1e-5
COLSUM_EPS = 1e-7

LN1_W, LN1_B, Q_B, K_B, V_B, LN2_W, LN2_B = range(0, 14, 2)
FC_B = 14
L0_BV, L0_BT = 22, 23
VEC_ROWS = 24


def xattn_two_layers(nc, A, out):
    B, C, D = A["x"].shape
    H = 16
    HD = D // H
    FF = A["L1_xattn_fc_w"].shape[1]
    HALVES = 2
    PAIRS = B // 2 // HALVES
    TOK = PAIRS * P
    G = D // P
    J = P // (2 * HD)
    HP = G * J
    M = FF // P
    SCALE = float(HD) ** -0.5

    PER_HALF = dict(
        ctx_turned=PAIRS, ctx_ready=PAIRS, keys_made=G, keys_ready=2 * G, values_made=PAIRS, values_ready=4 * PAIRS,
        gx_made=PAIRS, gx_ready=PAIRS, u_made=PAIRS, u_ready=PAIRS, energy_made=2 * PAIRS, energy_max=2 * PAIRS,
        energy_exp=4 * PAIRS, rowsum_inv=2 * PAIRS, scaled_u=4 * PAIRS, mixed=2 * PAIRS, colsum_ln=2 * PAIRS,
        colsum_inv=PAIRS, mix_normed=2 * PAIRS, relu_in=PAIRS, relu_out=PAIRS, x1_ready=PAIRS, x1_stats=PAIRS,
        x1_meanvar=PAIRS, x1_lnvar=PAIRS, x1_rstd=PAIRS, x1_normed=PAIRS, x1_turned=PAIRS, x1t_ready=2 * PAIRS,
        queries_made=G, queries_ready=G, x1_plus_bias=PAIRS,
        scores_made=PAIRS, scores_masked=PAIRS, scores_max=PAIRS, scores_shifted=PAIRS, probs_exp=PAIRS,
        probs_sum=PAIRS, probs_inv=PAIRS, probs_ready=PAIRS, probs_turned=PAIRS, probst_ready=2 * PAIRS,
        heads_made=PAIRS, heads_ready=2 * PAIRS, attn_made=PAIRS, hidden_ready=PAIRS, hid_stats=PAIRS,
        hid_meanvar=PAIRS, hid_lnvar=PAIRS, hid_rstd=PAIRS, hid_normed=PAIRS, hid_turned=PAIRS, hidt_ready=2 * PAIRS,
        hid_plus_bias=PAIRS, fc_made=M, gelu_ready=M, proj_made=PAIRS, out_ready=PAIRS,
    )

    with ExitStack() as ctx:
        def sb(name, shape, dt=F32):
            return ctx.enter_context(nc.sbuf_tensor(name, shape, dt))

        def sem(name):
            return ctx.enter_context(nc.semaphore(name))

        wqk = sb("wqk", [P, P])
        wv0 = sb("wv0", [P, P])
        wt0 = sb("wt0", [P, P])
        gram = sb("gram", [P, P])
        wtT = sb("wtT", [P, P])
        wtvT = sb("wtvT", [P, P])
        bv_cols = sb("bv_cols", [P, P])
        wtbv = sb("wtbv", [P, P])
        ident = sb("ident", [P, P])
        ones = sb("ones", [P, P])
        vec_rows = sb("vec_rows", [VEC_ROWS, P])
        vec = sb("vec", [P, VEC_ROWS])
        parity = sb("parity", [P, 2])
        wq = sb("wq", [P, G, D])
        wk = sb("wk", [P, G, D])
        wv = sb("wv", [P, G, D])
        wc = sb("wc", [P, G, D])
        wfc = sb("wfc", [P, G, FF])
        wpj = sb("wpj", [P, M, D])
        cproj_b = sb("cproj_b", [P, D])
        proj_b = sb("proj_b", [P, D])
        mask8 = sb("mask8", [P, HALVES * PAIRS, C], U8)
        maskadd = sb("maskadd", [P, HALVES * PAIRS, C])

        xs = sb("xs", [P, PAIRS, D])
        ys = sb("ys", [P, PAIRS, D])
        ctxT = sb("ctxT", [P, G, TOK])
        keys = sb("keys", [P, G, 2, TOK])
        vals = sb("vals", [P, PAIRS, 2, HP, 2 * HD])
        gx = sb("gx", [P, 2, D])
        uext = sb("uext", [P, 2, 2, 3 * C])
        us = sb("us", [P, 2, 2, P])
        att = sb("att", [P, 2, 2, D])
        nmax = sb("nmax", [P, 2, 2])
        rsum = sb("rsum", [P, 2, 2])
        rinv = sb("rinv", [P, 2, 2])
        csln = sb("csln", [P, D])
        csinv = sb("csinv", [P, D])
        mixn = sb("mixn", [P, D])
        rin = sb("rin", [P, D])
        rout = sb("rout", [P, D])
        x1 = sb("x1", [P, PAIRS, D])
        x1b = sb("x1b", [P, PAIRS, D])
        stats = sb("stats", [P, 6])
        mv = sb("mv", [P, 2])
        lnv = sb("lnv", [P, 1])
        rstd = sb("rstd", [P, 1])
        xn = sb("xn", [P, D])
        x1T = sb("x1T", [P, G, TOK])
        queries = sb("queries", [P, G, TOK])
        sc = sb("sc", [P, 2, 2 * BANK])
        smax = sb("smax", [P, 2, H])
        pr = sb("pr", [P, 2, 2 * BANK])
        psums = sb("psums", [P, 2, H])
        pinv = sb("pinv", [P, 2, H])
        pn = sb("pn", [P, 2, 2 * BANK])
        prT = sb("prT", [P, HP, P])
        hdT = sb("hdT", [P, G, P])
        hid = sb("hid", [P, PAIRS, D])
        hidb = sb("hidb", [P, PAIRS, D])
        hstats = sb("hstats", [P, 6])
        hmv = sb("hmv", [P, 2])
        hlnv = sb("hlnv", [P, 1])
        hrstd = sb("hrstd", [P, 1])
        hn = sb("hn", [P, D])
        hidT = sb("hidT", [P, G, TOK])
        ff = sb("ff", [P, M, TOK])
        res = sb("res", [P, PAIRS, D])

        psum = ctx.enter_context(nc.psum_tensor("psum", [P, 8, BANK], F32))

        l0w_loaded, vec_loaded, x_loaded, y_loaded = map(sem, ("l0w_loaded", "vec_loaded", "x_loaded", "y_loaded"))
        w_loaded = {k: sem("w_loaded_" + k) for k in ("k", "v", "q", "c", "fc", "pj", "cb", "pb", "mask")}
        diag_zeroed, ones_ready, ident_ready, zeros_ready = map(sem, ("diag_zeroed", "ones_ready", "ident_ready",
                                                                      "zeros_ready"))
        setup_pe, setup_dve, mask_ready, parity_ready = map(sem, ("setup_pe", "setup_dve", "mask_ready", "parity_ready"))
        stored = sem("stored")
        S = {k: sem(k) for k in PER_HALF}

        def wait(eng, h, name, count):
            eng.wait_ge(S[name], h * PER_HALF[name] + count)

        def bank(n):
            return psum[:, n, :]

        def halfbank(n, k):
            return psum[:, n, k * D:(k + 1) * D]

        def col(i):
            return vec[:, i:i + 1]

        def dram_half(t, h):
            n = 2 * PAIRS
            return t[bass.ds(h * n, n)].rearrange("(n e) c m -> (e c) n m", e=2)

        scores_ps = psum[:, 0:J, 0:G * P]
        probsT_ps = psum[:, 4:6, :].rearrange("p a (b t) -> p (a b) t", t=P)

        block = ctx.enter_context(nc.Block())

        @block.sync
        def _(sp):
            def load(t, dst, h, s):
                sp.dma_start(dst[:], dram_half(A[t], h)).then_inc(s, 16)

            load("x", xs, 0, x_loaded)
            sp.wait_ge(diag_zeroed, 1)
            for name, w in (("w_qk", wqk), ("w_v", wv0), ("w_t", wt0)):
                for e in range(2):
                    sp.dma_start(w[e * C:(e + 1) * C, e * C:(e + 1) * C], A["L0_xattn_" + name]).then_inc(l0w_loaded, 16)
            for name, w, s in (("q_w", wq, "q"), ("cproj_w", wc, "c"), ("fc_w", wfc, "fc"), ("proj_w", wpj, "pj")):
                sp.dma_start(w[:], A["L1_xattn_" + name].rearrange("(g p) n -> p g n", p=P)).then_inc(w_loaded[s], 16)
            sp.wait_ge(S["ctx_turned"], PAIRS)
            sp.wait_ge(S["energy_made"], 2 * PAIRS)
            load("ctx_2048", ys, 1, y_loaded)
            sp.wait_ge(S["x1_ready"], PAIRS)
            sp.wait_ge(S["u_made"], PAIRS)
            load("x", xs, 1, x_loaded)
            for h in range(HALVES):
                for n in range(PAIRS):
                    wait(sp, h, "out_ready", n + 1)
                    sp.dma_start(dram_half(out, h)[:, n, :], res[:, n, :]).then_inc(stored, 16)
            sp.wait_ge(stored, HALVES * PAIRS * 16)

        @block.gpsimd
        def _(pool):
            pool.memset(ones[:], 1.0).then_inc(ones_ready, 1)
            pool.wait_ge(ones_ready, 1)
            pool.affine_select(out=ident[:], in_=ones[:], compare_op=ALU.is_equal, fill=0.0, base=0,
                               pattern=[[-1, P]], channel_multiplier=1).then_inc(ident_ready, 1)
            pool.memset(uext[:], 1.0).then_inc(zeros_ready, 1)
            pool.memset(vals[:], 0.0).then_inc(zeros_ready, 1)
            for h in range(HALVES):
                for n in range(PAIRS):
                    wait(pool, h, "relu_out", n + 1)
                    pool.tensor_tensor(x1[:, n, :], xs[:, n, :], rout[:], ALU.add).then_inc(S["x1_ready"], 1)
                for n in range(PAIRS):
                    if n == 0:
                        pool.wait_ge(w_loaded["cb"], 16)
                        pool.wait_ge(w_loaded["pb"], 16)
                        wait(pool, h, "x1_ready", PAIRS)
                    pool.tensor_tensor(x1b[:, n, :], x1[:, n, :], cproj_b[:], ALU.add).then_inc(S["x1_plus_bias"], 1)
                for n in range(PAIRS + 2):
                    if n < PAIRS:
                        s = n % 2
                        wait(pool, h, "probs_inv", n + 1)
                        if n >= 2:
                            wait(pool, h, "probs_turned", n - 1)
                        pool.tensor_tensor(pn[:, s, :].rearrange("p (h k) -> p h k", h=H),
                                           pr[:, s, :].rearrange("p (h k) -> p h k", h=H),
                                           pinv[:, s, :].unsqueeze(2).broadcast_to([P, H, C]),
                                           ALU.mult).then_inc(S["probs_ready"], 1)
                    if n >= 2:
                        wait(pool, h, "hidden_ready", n - 1)
                        pool.tensor_tensor(hidb[:, n - 2, :], hid[:, n - 2, :], proj_b[:],
                                           ALU.add).then_inc(S["hid_plus_bias"], 1)

        @block.scalar
        def _(act):
            act.dma_start(ys[:], dram_half(A["ctx_2048"], 0)).then_inc(y_loaded, 16)
            for name, at in (("ln1_w", LN1_W), ("ln1_b", LN1_B), ("q_b", Q_B), ("k_b", K_B), ("v_b", V_B),
                             ("ln2_w", LN2_W), ("ln2_b", LN2_B), ("fc_b", FC_B)):
                v = A["L1_xattn_" + name]
                rows = v.shape[0] // P
                act.dma_start(vec_rows[at:at + rows, :], v.rearrange("(r p) -> r p", p=P)).then_inc(vec_loaded, 16)
            for name, at in (("b_v", L0_BV), ("b_t", L0_BT)):
                for e in range(2):
                    act.dma_start(vec_rows[at:at + 1, e * C:(e + 1) * C],
                                  A["L0_xattn_" + name].rearrange("(r p) -> r p", r=1)).then_inc(vec_loaded, 16)
            for name, w, s in (("k_w", wk, "k"), ("v_w", wv, "v")):
                act.dma_start(w[:], A["L1_xattn_" + name].rearrange("(g p) n -> p g n", p=P)).then_inc(w_loaded[s], 16)
            for name, w, s in (("cproj_b", cproj_b, "cb"), ("proj_b", proj_b, "pb")):
                act.dma_start(w[:], A["L1_xattn_" + name].rearrange("(o d) -> o d", o=1).broadcast_to([P, D])
                              ).then_inc(w_loaded[s], 16)
            for e in range(2):
                src = A["mask_BxS2_bf1"].rearrange("(n e) k -> e n k", e=2)[e:e + 1].broadcast_to([C, B // 2, C])
                act.dma_start(mask8[e * C:(e + 1) * C, :, :], src).then_inc(w_loaded["mask"], 16)

            def identity(dst, src, bias, scale, done):
                act.activation(dst, src, ACT.Identity, bias=bias, scale=scale).then_inc(S[done], 1)

            for h in range(HALVES):
                act.add_instruction(mybir.InstLoadActFuncSet(name=nc.get_next_instruction_name(),
                                                             act_func_set_id=EXP_LN_SET, ins=[], outs=[]))
                for n in range(PAIRS):
                    wait(act, h, "ctx_turned", n + 1)
                    act.copy(ctxT[:, :, n * P:(n + 1) * P],
                             halfbank(n % 2, 0).rearrange("p (g t) -> p g t", g=G)).then_inc(S["ctx_ready"], 1)

                def energy_exp(n, e):
                    k = 2 * n + e
                    wait(act, h, "energy_max", k + 1)
                    if k >= 2:
                        wait(act, h, "mixed", k - 1)
                        wait(act, h, "rowsum_inv", k - 1)
                    for j in range(2):
                        act.activation(att[:, e, j, :], halfbank(3 + e, j), ACT.Exp, bias=nmax[:, e, j:j + 1],
                                       accum_out=rsum[:, e, j:j + 1]).then_inc(S["energy_exp"], 1)

                def colsum_ln(n, e):
                    wait(act, h, "mixed", 2 * n + e + 1)
                    act.activation(csln[e * C:(e + 1) * C, :],
                                   psum[(1 - e) * C:(2 - e) * C, 5 + e, 0:D], ACT.Ln,
                                   bias=COLSUM_EPS).then_inc(S["colsum_ln"], 1)

                for n in range(PAIRS + 1):
                    if n < PAIRS:
                        energy_exp(n, 0)
                    if n >= 1:
                        colsum_ln(n - 1, 1)
                        wait(act, h, "colsum_ln", 2 * n)
                        act.activation(csinv[:], csln[:], ACT.Exp, scale=-1.0).then_inc(S["colsum_inv"], 1)
                    if n < PAIRS:
                        energy_exp(n, 1)
                    if n >= 1:
                        wait(act, h, "relu_in", n)
                        act.activation(rout[:], rin[:], ACT.Relu, bias=col(L0_BT)).then_inc(S["relu_out"], 1)
                        wait(act, h, "x1_meanvar", n)
                        act.activation(lnv[:], mv[:, 1:2], ACT.Ln, bias=LN_EPS).then_inc(S["x1_lnvar"], 1)
                        wait(act, h, "x1_lnvar", n)
                        act.activation(rstd[:], lnv[:], ACT.Exp, scale=-0.5).then_inc(S["x1_rstd"], 1)
                    if n < PAIRS:
                        colsum_ln(n, 0)
                    if n >= 1:
                        wait(act, h, "x1_turned", n)
                        for g in range(G):
                            identity(x1T[:, g, (n - 1) * P:n * P], psum[:, 7, g * P:(g + 1) * P],
                                     col(LN1_B + g), col(LN1_W + g), "x1t_ready")
                for g in range(G):
                    wait(act, h, "queries_made", g + 1)
                    identity(queries[:, g, :], bank(4 + g), col(Q_B + g), 1.0, "queries_ready")

                for n in range(-1, PAIRS + 2):
                    if 0 <= n - 2 < PAIRS:
                        wait(act, h, "hid_turned", n - 1)
                        for g in range(G):
                            identity(hidT[:, g, (n - 2) * P:(n - 1) * P], psum[:, 7, g * P:(g + 1) * P],
                                     col(LN2_B + g), col(LN2_W + g), "hidt_ready")
                    if 0 <= n - 1 < PAIRS:
                        wait(act, h, "heads_made", n)
                        for g in range(G):
                            identity(hdT[:, g, :], psum[:, 6, g * P:(g + 1) * P], col(V_B + g), 1.0, "heads_ready")
                    if 0 <= n + 1 < PAIRS:
                        s = (n + 1) % 2
                        wait(act, h, "scores_shifted", n + 2)
                        if n + 1 >= 2:
                            wait(act, h, "probs_ready", n)
                        act.activation(pr[:, s, :], sc[:, s, :], ACT.Exp, scale=SCALE).then_inc(S["probs_exp"], 1)
                    if 0 <= n - 1 < PAIRS:
                        wait(act, h, "hid_meanvar", n)
                        act.activation(hlnv[:], hmv[:, 1:2], ACT.Ln, bias=LN_EPS).then_inc(S["hid_lnvar"], 1)
                        wait(act, h, "hid_lnvar", n)
                        act.activation(hrstd[:], hlnv[:], ACT.Exp, scale=-0.5).then_inc(S["hid_rstd"], 1)
                    if 0 <= n < PAIRS:
                        wait(act, h, "probs_turned", n + 1)
                        act.copy(prT[:, 0:HP // 2, :].rearrange("p a t -> p (a t)"),
                                 bank(4)).then_inc(S["probst_ready"], 1)

                for m in range(M):
                    wait(act, h, "fc_made", m + 1)
                    act.activation(ff[:, m, :], bank(m % 4), ACT.Gelu_apprx_tanh,
                                   bias=col(FC_B + m)).then_inc(S["gelu_ready"], 1)

        @block.vector
        def _(dve):
            for n, w in enumerate((wqk, wv0, wt0)):
                ins = dve.memset(w[:], 0.0)
            ins.then_inc(diag_zeroed, 1)
            dve.wait_ge(setup_pe, 1)
            dve.tensor_copy(vec[:], psum[:, 7, 0:VEC_ROWS]).then_inc(setup_dve, 1)
            dve.wait_ge(setup_pe, 2)
            dve.tensor_copy(wtT[:], psum[:, 6, 0:P]).then_inc(setup_dve, 1)
            dve.wait_ge(setup_dve, 2)
            dve.wait_ge(ident_ready, 1)
            dve.tensor_scalar(bv_cols[:], ones[:], col(L0_BV), None, ALU.mult).then_inc(setup_dve, 1)
            dve.tensor_reduce(parity[:], ident[:].rearrange("p (j a d) -> p a j d", a=2, d=HD), AX.XY,
                              ALU.add).then_inc(parity_ready, 1)
            dve.wait_ge(setup_pe, 3)
            dve.tensor_copy(gram[:], psum[:, 5, 0:P]).then_inc(setup_dve, 1)
            dve.tensor_copy(wtvT[:], psum[:, 5, P:2 * P]).then_inc(setup_dve, 1)
            dve.tensor_copy(wtbv[:], psum[:, 5, 2 * P:3 * P]).then_inc(setup_dve, 1)
            dve.wait_ge(w_loaded["mask"], 32)
            dve.tensor_scalar(maskadd[:], mask8[:], -1.0, -FLOAT_MIN, ALU.add, ALU.mult).then_inc(mask_ready, 1)
            dve.wait_ge(zeros_ready, 2)
            dve.wait_ge(parity_ready, 1)

            def mean_var(h, src, st, agg, name):
                dve.bn_stats(st[:], src).then_inc(S[name + "_stats"], 1)

            for h in range(HALVES):
                for g in range(G):
                    wait(dve, h, "keys_made", g + 1)
                    for a in range(2):
                        dve.tensor_scalar(keys[:, g, a, :], bank(2 + g), col(K_B + g), parity[:, a:a + 1],
                                          ALU.add, ALU.mult).then_inc(S["keys_ready"], 1)
                for n in range(PAIRS):
                    wait(dve, h, "values_made", n + 1)
                    for e in range(2):
                        src = psum[e * C:(e + 1) * C, 4 + n % 2, 0:D].rearrange("p (i a d) -> p i a d", a=2, d=HD)
                        for a in range(2):
                            dve.tensor_copy(vals[a * C:(a + 1) * C, n, e, :, a * HD:(a + 1) * HD],
                                            src[:, :, a, :]).then_inc(S["values_ready"], 1)

                def energy_max(n, e):
                    wait(dve, h, "energy_made", 2 * n + e + 1)
                    if 2 * n + e >= 2:
                        wait(dve, h, "energy_exp", 2 * (2 * n + e - 1))
                    dve.tensor_reduce(nmax[:, e, :], bank(3 + e).rearrange("p (j m) -> p j m", j=2), AX.X, ALU.max,
                                      negate=True).then_inc(S["energy_max"], 1)

                def scale_u(n, e):
                    k = 2 * n + e
                    wait(dve, h, "energy_exp", 2 * k + 2)
                    dve.reciprocal(rinv[:, e, :], rsum[:, e, :]).then_inc(S["rowsum_inv"], 1)
                    wait(dve, h, "rowsum_inv", k + 1)
                    wait(dve, h, "u_ready", n + 1)
                    if k >= 2:
                        wait(dve, h, "mixed", k - 1)
                    for j in range(2):
                        dve.tensor_scalar(us[:, e, j, :], uext[:, n % 2, j, e * C:e * C + P], rinv[:, e, j:j + 1], None,
                                          ALU.mult).then_inc(S["scaled_u"], 1)

                def take_gx(n):
                    wait(dve, h, "gx_made", n + 1)
                    dve.tensor_copy(gx[:, n % 2, :], halfbank(n % 2, 0)).then_inc(S["gx_ready"], 1)

                def take_u(n):
                    wait(dve, h, "u_made", n + 1)
                    if n >= 2:
                        wait(dve, h, "scaled_u", 4 * (n - 1))
                    for e in range(1):
                        dst = uext[:, n % 2, :, :].rearrange("p j (b c) -> p j b c", b=3)[:, :, 0:3:2, :]
                        dve.tensor_tensor(dst, halfbank(2, 0).rearrange("p (j b c) -> p j b c", j=2, b=2),
                                          wtbv[:].rearrange("p (b c) -> p b c", b=2).unsqueeze(1)
                                          .broadcast_to([P, 2, 2, C]), ALU.add).then_inc(S["u_ready"], 1)

                for n in range(-1, PAIRS + 1):
                    if 0 <= n < PAIRS:
                        energy_max(n, 0)
                    if 0 <= n - 1:
                        wait(dve, h, "colsum_inv", n)
                        for e in range(2):
                            dve.tensor_tensor(mixn[e * C:(e + 1) * C, :],
                                              psum[e * C:(e + 1) * C, 5 + e, 0:D],
                                              csinv[e * C:(e + 1) * C, :], ALU.mult).then_inc(S["mix_normed"], 1)
                        wait(dve, h, "mix_normed", 2 * n)
                        if n >= 2:
                            wait(dve, h, "relu_out", n - 1)
                        dve.tensor_tensor(rin[:], halfbank((n - 1) % 2, 1), mixn[:],
                                          ALU.subtract).then_inc(S["relu_in"], 1)
                    if 0 <= n < PAIRS:
                        energy_max(n, 1)
                        scale_u(n, 0)
                    if n + 1 < PAIRS:
                        take_gx(n + 1)
                    if 0 <= n - 1:
                        wait(dve, h, "x1_ready", n)
                        dve.bn_stats(stats[:], x1[:, n - 1, :]).then_inc(S["x1_stats"], 1)
                        wait(dve, h, "x1_stats", n)
                        dve.wait_ge(mask_ready, 1)
                        dve.bn_aggr(mv[:], stats[:]).then_inc(S["x1_meanvar"], 1)
                    if n + 1 < PAIRS:
                        take_u(n + 1)
                    if 0 <= n - 1:
                        wait(dve, h, "x1_rstd", n)
                        if n >= 2:
                            wait(dve, h, "x1_turned", n - 1)
                        dve.tensor_scalar(xn[:], x1[:, n - 1, :], mv[:, 0:1], rstd[:, 0:1], ALU.subtract,
                                          ALU.mult).then_inc(S["x1_normed"], 1)
                    if 0 <= n < PAIRS:
                        scale_u(n, 1)

                def heads(t, s):
                    return t[:, s, :].rearrange("p (h k) -> p h k", h=H)

                for n in range(-1, PAIRS + 2):
                    if 0 <= n + 1 < PAIRS:
                        s = (n + 1) % 2
                        wait(dve, h, "scores_made", n + 2)
                        if n == -1:
                            dve.wait_ge(mask_ready, 1)
                        if n + 1 >= 2:
                            wait(dve, h, "probs_exp", n)
                        dve.tensor_tensor(
                            sc[:, s, :].rearrange("p (j i k) -> p j i k", j=J, k=C),
                            scores_ps.rearrange("p j (i k) -> p j i k", k=C),
                            maskadd[:, bass.ds(h * PAIRS + (n + 1), 1), :].unsqueeze(1).broadcast_to([P, J, H // J, C]),
                            ALU.add).then_inc(S["scores_masked"], 1)
                        wait(dve, h, "scores_masked", n + 2)
                        dve.tensor_reduce(smax[:, s, :], heads(sc, s), AX.X, ALU.max).then_inc(S["scores_max"], 1)
                        wait(dve, h, "scores_max", n + 2)
                        dve.tensor_tensor(heads(sc, s), heads(sc, s), smax[:, s, :].unsqueeze(2).broadcast_to([P, H, C]),
                                          ALU.subtract).then_inc(S["scores_shifted"], 1)
                    if 0 <= n - 1 < PAIRS:
                        wait(dve, h, "attn_made", n)
                        wait(dve, h, "x1_plus_bias", n)
                        dve.tensor_tensor(hid[:, n - 1, :], halfbank(7, 0), x1b[:, n - 1, :],
                                          ALU.add).then_inc(S["hidden_ready"], 1)
                        wait(dve, h, "hidden_ready", n)
                        dve.bn_stats(hstats[:], hid[:, n - 1, :]).then_inc(S["hid_stats"], 1)
                        wait(dve, h, "hid_stats", n)
                        dve.wait_ge(mask_ready, 1)
                        dve.bn_aggr(hmv[:], hstats[:]).then_inc(S["hid_meanvar"], 1)
                    if 0 <= n + 1 < PAIRS:
                        wait(dve, h, "probs_exp", n + 2)
                        dve.tensor_reduce(psums[:, s, :], heads(pr, s), AX.X, ALU.add).then_inc(S["probs_sum"], 1)
                        wait(dve, h, "probs_sum", n + 2)
                        if n + 1 >= 2:
                            wait(dve, h, "probs_ready", n)
                        dve.reciprocal(pinv[:, s, :], psums[:, s, :]).then_inc(S["probs_inv"], 1)
                    if 0 <= n < PAIRS:
                        wait(dve, h, "probs_turned", n + 1)
                        dve.tensor_copy(prT[:, HP // 2:HP, :].rearrange("p a t -> p (a t)"),
                                        bank(5)).then_inc(S["probst_ready"], 1)
                    if 0 <= n - 1 < PAIRS:
                        wait(dve, h, "hid_rstd", n)
                        if n - 1 >= 1:
                            wait(dve, h, "hid_turned", n - 1)
                        dve.tensor_scalar(hn[:], hid[:, n - 1, :], hmv[:, 0:1], hrstd[:, 0:1], ALU.subtract,
                                          ALU.mult).then_inc(S["hid_normed"], 1)

                for n in range(PAIRS):
                    wait(dve, h, "proj_made", n + 1)
                    wait(dve, h, "hid_plus_bias", n + 1)
                    if n == 0:
                        dve.wait_ge(stored, h * (16 * PAIRS))
                    dve.tensor_tensor(res[:, n, :], halfbank(4 + n, 0), hidb[:, n, :],
                                      ALU.add).then_inc(S["out_ready"], 1)

        @block.tensor
        def _(pe):
            def mm(dst, lhsT, rhs, start=True, stop=True):
                return pe.matmul(dst, lhsT, rhs, start=start, stop=stop)

            pe.wait_ge(ident_ready, 1)
            pe.wait_ge(vec_loaded, 12 * 16)
            pe.transpose(psum[:, 7, 0:VEC_ROWS], vec_rows[:], ident[0:VEC_ROWS, 0:VEC_ROWS]).then_inc(setup_pe, 1)
            pe.wait_ge(l0w_loaded, 6 * 16)
            pe.transpose(psum[:, 6, 0:P], wt0[:], ident[:]).then_inc(setup_pe, 1)
            mm(psum[:, 5, 0:P], wqk[:], wqk[:])
            pe.wait_ge(setup_dve, 3)
            mm(psum[:, 5, P:2 * P], wv0[:], wtT[:])
            mm(psum[:, 5, 2 * P:3 * P], bv_cols[:], wtT[:]).then_inc(setup_pe, 1)
            pe.wait_ge(setup_dve, 6)

            for h in range(HALVES):
                pe.wait_ge(y_loaded, (h + 1) * 16)
                for n in range(PAIRS):
                    if n >= 2:
                        wait(pe, h, "ctx_ready", n - 1)
                    for g in range(G):
                        ins = pe.transpose(psum[:, n % 2, g * P:(g + 1) * P], ys[:, n, g * P:(g + 1) * P], ident[:])
                    ins.then_inc(S["ctx_turned"], 1)
                wait(pe, h, "ctx_ready", PAIRS)
                pe.wait_ge(w_loaded["k"], 16)
                for g in range(G):
                    for k in range(G):
                        ins = mm(bank(2 + g), wk[:, k, g * P:(g + 1) * P], ctxT[:, k, :], k == 0, k == G - 1)
                    ins.then_inc(S["keys_made"], 1)
                pe.wait_ge(w_loaded["v"], 16)
                wait(pe, h, "out_ready", 0)
                for n in range(PAIRS):
                    if n >= 2:
                        wait(pe, h, "values_ready", 4 * (n - 1))
                    for k in range(G):
                        ins = mm(halfbank(4 + n % 2, 0), ctxT[:, k, n * P:(n + 1) * P], wv[:, k, :], k == 0, k == G - 1)
                    ins.then_inc(S["values_made"], 1)

                def project(n):
                    if n >= 2:
                        wait(pe, h, "relu_in", n - 1)
                    mm(halfbank(n % 2, 0), gram[:], xs[:, n, :])
                    mm(halfbank(n % 2, 1), wtT[:], xs[:, n, :]).then_inc(S["gx_made"], 1)
                    if n >= 1:
                        wait(pe, h, "u_ready", n)
                    for j in range(2):
                        ins = mm(psum[:, 2, j * P:(j + 1) * P], xs[:, n, j * P:(j + 1) * P], wtvT[:])
                    ins.then_inc(S["u_made"], 1)

                def energy(n, e):
                    k = 2 * n + e
                    if k >= 2:
                        wait(pe, h, "energy_exp", 2 * (k - 1))
                    rows = slice(e * C, (e + 1) * C)
                    for j in range(2):
                        ins = mm(halfbank(3 + e, j), ys[rows, n, j * P:(j + 1) * P], gx[rows, n % 2, :])
                    ins.then_inc(S["energy_made"], 1)

                def mix(n, e):
                    k = 2 * n + e
                    wait(pe, h, "scaled_u", 2 * k + 2)
                    if n >= 1:
                        wait(pe, h, "mix_normed", 2 * (n - 1) + e + 1)
                    for j in range(2):
                        ins = mm(halfbank(5 + e, 0), us[:, e, j, :], att[:, e, j, :], j == 0, j == 1)
                    ins.then_inc(S["mixed"], 1)

                pe.wait_ge(x_loaded, (h + 1) * 16)
                wait(pe, h, "keys_ready", 2 * G)
                project(0)
                wait(pe, h, "values_ready", 4 * PAIRS)
                for n in range(PAIRS + 1):
                    if n < PAIRS:
                        wait(pe, h, "gx_ready", n + 1)
                        energy(n, 0)
                    if n >= 1:
                        mix(n - 1, 1)
                    if n < PAIRS:
                        energy(n, 1)
                    if n + 1 < PAIRS:
                        project(n + 1)
                    if n < PAIRS:
                        mix(n, 0)
                    if n >= 1:
                        wait(pe, h, "x1_normed", n)
                        if n >= 2:
                            wait(pe, h, "x1t_ready", 2 * (n - 1))
                        for g in range(G):
                            ins = pe.transpose(psum[:, 7, g * P:(g + 1) * P], xn[:, g * P:(g + 1) * P], ident[:])
                        ins.then_inc(S["x1_turned"], 1)

                pe.wait_ge(w_loaded["q"], 16)
                wait(pe, h, "x1t_ready", 2 * PAIRS)
                for g in range(G):
                    for k in range(G):
                        ins = mm(bank(4 + g), wq[:, k, g * P:(g + 1) * P], x1T[:, k, :], k == 0, k == G - 1)
                    ins.then_inc(S["queries_made"], 1)
                wait(pe, h, "queries_ready", G)
                pe.wait_ge(w_loaded["c"], 16)

                for n in range(-1, PAIRS + 2):
                    if 0 <= n + 1 < PAIRS:
                        s = (n + 1) % 2
                        if n + 1 >= 1:
                            wait(pe, h, "scores_masked", n + 1)
                        for g in range(G):
                            for e in range(2):
                                t = slice((n + 1) * P + e * C, (n + 1) * P + (e + 1) * C)
                                for j in range(J):
                                    r = slice(32 * j, 32 * (j + 1))
                                    ins = mm(scores_ps[e * C:(e + 1) * C, j, g * P:(g + 1) * P],
                                             queries[r, g, t], keys[r, g, :, t])
                        ins.then_inc(S["scores_made"], 1)
                    if 0 <= n - 2 < PAIRS:
                        wait(pe, h, "hid_normed", n - 1)
                        if n - 2 >= 1:
                            wait(pe, h, "hidt_ready", 2 * (n - 2))
                        for g in range(G):
                            ins = pe.transpose(psum[:, 7, g * P:(g + 1) * P], hn[:, g * P:(g + 1) * P], ident[:])
                        ins.then_inc(S["hid_turned"], 1)
                    if 0 <= n - 1 < PAIRS:
                        wait(pe, h, "probst_ready", 2 * n)
                        if n - 1 >= 1:
                            wait(pe, h, "heads_ready", 2 * (n - 1))
                        for e in range(2):
                            for g in range(G):
                                for j in range(J):
                                    ins = mm(psum[32 * j:32 * (j + 1), 6, g * P + e * C:g * P + (e + 1) * C],
                                             vals[:, n - 1, e, g * J + j, :], prT[:, j * G + g, e * C:(e + 1) * C])
                        ins.then_inc(S["heads_made"], 1)
                        wait(pe, h, "heads_ready", 2 * n)
                        if n - 1 >= 1:
                            wait(pe, h, "hidt_ready", 2 * (n - 1))
                        for k in range(G):
                            ins = mm(halfbank(7, 0), hdT[:, k, :], wc[:, k, :], k == 0, k == G - 1)
                        ins.then_inc(S["attn_made"], 1)
                    if 0 <= n < PAIRS:
                        wait(pe, h, "probs_ready", n + 1)
                        if n >= 1:
                            wait(pe, h, "probst_ready", 2 * n)
                        for i in range(HP):
                            ins = pe.transpose(probsT_ps[:, i, :], pn[:, n % 2, i * P:(i + 1) * P], ident[:])
                        ins.then_inc(S["probs_turned"], 1)

                wait(pe, h, "hidt_ready", 2 * PAIRS)
                pe.wait_ge(w_loaded["fc"], 16)
                for m in range(M):
                    if m >= 4:
                        wait(pe, h, "gelu_ready", m - 3)
                    for k in range(G):
                        ins = mm(bank(m % 4), wfc[:, k, m * P:(m + 1) * P], hidT[:, k, :], k == 0, k == G - 1)
                    ins.then_inc(S["fc_made"], 1)
                pe.wait_ge(w_loaded["pj"], 16)
                for n in range(PAIRS):
                    for m in range(M):
                        if n == 0:
                            wait(pe, h, "gelu_ready", m + 1)
                        ins = mm(halfbank(4 + n, 0), ff[:, m, n * P:(n + 1) * P], wpj[:, m, :], m == 0, m == M - 1)
                    ins.then_inc(S["proj_made"], 1)


_OUT = ((16, 64, 256), "float32")


def kernel(**inputs):
    import numpy as _np
    import concourse.bacc as _bacc
    from concourse import mybir as _mybir
    from concourse.bass_utils import run_bass_kernel_spmd as _run

    nc = _bacc.Bacc("TRN2", target_bir_lowering=False, num_devices=1)
    arrays, aps = {}, {}
    for name, a in inputs.items():
        a = _np.ascontiguousarray(a)
        if a.dtype == _np.bool_:
            a = a.view(_np.uint8)
        arrays[f"in_{name}_dram"] = a
        aps[name] = nc.dram_tensor(f"in_{name}_dram", a.shape, _mybir.dt.from_np(a.dtype), kind="ExternalInput").ap()
    out = nc.dram_tensor("out_0_dram", _OUT[0], _mybir.dt.from_np(_np.dtype(_OUT[1])), kind="ExternalOutput").ap()
    xattn_two_layers(nc, aps, out)
    r = _run(nc, [arrays], core_ids=[0])
    return r.results[0]["out_0_dram"]
```

```python
from contextlib import ExitStack

import concourse.bass as bass
from concourse import mybir

F32 = mybir.dt.float32
F32R = mybir.dt.float32r
U8 = mybir.dt.uint8
ALU = mybir.AluOpType
ACT = mybir.ActivationFunctionType
AX = mybir.AxisListType

P = 128
BANK = 512
EXP_LN_SET = 6
FLOAT_MIN = -3.4028234663852886e38
LN_EPS = 1e-5
COLSUM_EPS = 1e-7

LN1_W, LN1_B, Q_B, K_B, V_B, LN2_W, LN2_B = range(0, 14, 2)
FC_B = 14
L0_BV, L0_BT = 22, 23
VEC_ROWS = 24


def xattn_two_layers(nc, A, out):
    B, C, D = A["x"].shape
    H = 16
    HD = D // H
    FF = A["L1_xattn_fc_w"].shape[1]
    N = B // 2
    HALVES = 2
    NH = N // HALVES
    TOK = NH * P
    G = D // P
    J = P // (2 * HD)
    HP = G * J
    M = FF // P
    SCALE = float(HD) ** -0.5
    W = 2 * BANK
    WPARTS = 2 * G * FF // W

    with ExitStack() as ctx:
        def sb(name, shape, dt=F32):
            return ctx.enter_context(nc.sbuf_tensor(name, shape, dt))

        def sem(name):
            return ctx.enter_context(nc.semaphore(name))

        wqk = sb("wqk", [P, C])
        wv0 = sb("wv0", [P, C])
        wt0 = sb("wt0", [P, C])
        gram = sb("gram", [P, P])
        wtT = sb("wtT", [P, P])
        wtvT = sb("wtvT", [P, P])
        bv_cols = sb("bv_cols", [P, P])
        wtbv = sb("wtbv", [P, P])
        ident = sb("ident", [P, P])
        ones = sb("ones", [P, P])
        vec0_rows = sb("vec0_rows", [VEC_ROWS - L0_BV, P])
        vec_rows = sb("vec_rows", [L0_BV, P])
        vec = sb("vec", [P, VEC_ROWS])
        parity = sb("parity", [P, 2])
        half_power = sb("half_power", [P, 1])
        wq = sb("wq", [P, G, D])
        wk = sb("wk", [P, G, D])
        wv = sb("wv", [P, G, D])
        wc = sb("wc", [P, G, D])
        wstage = sb("wstage", [P, W])
        wfc = [sb("wfc_hi", [P, G, FF], F32R), sb("wfc_lo", [P, G, FF], F32R)]
        wpj = [sb("wpj_hi", [P, M, D], F32R), sb("wpj_lo", [P, M, D], F32R)]
        cproj_b = sb("cproj_b", [P, D])
        proj_b = sb("proj_b", [P, D])
        mask8 = sb("mask8", [P, N, C], U8)
        maskadd = sb("maskadd", [P, N, C])

        rows = sb("rows", [P, N, D])
        ys = sb("ys", [P, N, D])
        ctxT = sb("ctxT", [P, G, TOK])
        keys = sb("keys", [P, G, 2, N * P])
        vals = sb("vals", [P, N, 2, HP, 2 * HD])
        gx = sb("gx", [P, 2, D])
        uext = sb("uext", [P, 2, 2, 3 * C])
        us = sb("us", [P, 2, 2, 2, P])
        att = sb("att", [P, 2, 2, 2, D])
        nmax = sb("nmax", [P, 2, 2, 2])
        rsum = sb("rsum", [P, 2, 2, 2])
        rinv = sb("rinv", [P, 2, 2, 2])
        csln = sb("csln", [P, D])
        csinv = sb("csinv", [P, D])
        mixn = sb("mixn", [P, D])
        rin = sb("rin", [P, 2, D])
        rout = sb("rout", [P, D])
        stats = sb("stats", [P, 6])
        mv = sb("mv", [P, 2, 2])
        vareps = sb("vareps", [P, 1])
        rstd = sb("rstd", [P, 1])
        xn = sb("xn", [P, 2, D])
        x1T = sb("x1T", [P, G, TOK])
        queries = sb("queries", [P, G, N * P])
        probs = sb("probs", [P, 2, G * BANK])
        smax = sb("smax", [P, H])
        psums = sb("psums", [P, 2, H])
        pinv = sb("pinv", [P, 2, H])
        prT = sb("prT", [P, HP, P])
        hdT = sb("hdT", [P, G, P])
        hn = sb("hn", [P, 2, D])
        hidf = sb("hidf", [P, G, P])
        hidT = [sb("hidT_hi", [P, G, N * P], F32R), sb("hidT_lo", [P, G, N * P], F32R)]
        act_ff = ys[:, 0:4, :].rearrange("p (k a) d -> p k (a d)", k=2)
        ff = [sb("ff_hi", [P, M, TOK], F32R), sb("ff_lo", [P, M, TOK], F32R)]

        psum = ctx.enter_context(nc.psum_tensor("psum", [P, 8, BANK], F32))
        PROJ0, ENERGY, MIX, WTX, TURN, FILL = 0, 1, 3, 5, 6, 7
        MLP_BANKS = [4, 5, 4, 5]
        SETUP_WT, SETUP_GRAM, SETUP_WTV, SETUP_VEC0, SETUP_WTBV, SETUP_VEC = 6, 5, 3, 4, 4, 6
        PROBST, HEADS = 4, 6

        wt_loaded, wqk_loaded, wv0_loaded = sem("wt_loaded"), sem("wqk_loaded"), sem("wv0_loaded")
        vec0_loaded, vec_loaded = sem("vec0_loaded"), sem("vec_loaded")
        x_loaded = [sem(f"x_loaded{i}") for i in range(3)]
        y_loaded = [sem(f"y_loaded{i}") for i in range(3)]
        w_loaded = {k: sem("w_loaded_" + k) for k in ("k", "v", "q", "c", "part", "cb", "pb", "mask")}
        diag_zeroed, ones_ready, ident_ready, zeros_ready = map(sem, ("diag_zeroed", "ones_ready", "ident_ready",
                                                                      "zeros_ready"))
        vec0_turned, vec0_ready, vec_turned, vec_ready, wt_turned, wt_ready = map(sem, (
            "vec0_turned", "vec0_ready", "vec_turned", "vec_ready", "wt_turned", "wt_ready"))
        bv_ready, gram_made, gram_ready, wtv_made, wtv_ready, wtbv_made, wtbv_ready = map(sem, (
            "bv_ready", "gram_made", "gram_ready", "wtv_made", "wtv_ready", "wtbv_made", "wtbv_ready"))
        mask_ready, parity_ready, stored = map(sem, ("mask_ready", "parity_ready", "stored"))
        S = {k: sem(k) for k in (
            "part_hi part_lo ctx_turned ctx_ready keys_made keys_ready values_made values_ready "
            "proj_made proj_ready energy_made energy_max energy_exp rowsum_inv scaled_u mixed wtx_made colsum_ln "
            "colsum_inv mix_normed relu_in relu_out x1_ready x1_stats x1_meanvar x1_vareps x1_rstd x1_normed x1_turned "
            "x1t_ready queries_made queries_ready x1_plus_bias scores_made scores_masked scores_max scores_shifted "
            "probs_exp probs_sum probs_inv probs_ready probs_turned probst_ready heads_made heads_ready attn_made "
            "hidden_ready hid_stats hid_meanvar hid_vareps hid_rstd hid_normed hid_turned hidf_ready hid_hi hid_lo "
            "hid_plus_bias fc_made gelu_ready ff_hi ff_lo mlp_made out_ready").split()}

        def wait(eng, name, count):
            if count > 0:
                eng.wait_ge(S[name], count)

        def bank(n):
            return psum[:, n, :]

        def halfbank(n, k):
            return psum[:, n, k * D:(k + 1) * D]

        def col(i):
            return vec[:, i:i + 1]

        def pairs(t, a, b):
            return t[2 * a:2 * b].rearrange("(n e) c m -> (e c) n m", e=2)

        LOADS = [(0, 1), (1, NH), (NH, N)]

        def landed(eng, sems, n):
            for (a, b), s in zip(LOADS, sems):
                if a <= n < b:
                    eng.wait_ge(s, 16)

        scores_ps = psum[:, 0:J, 0:G * P]
        probsT_ps = psum[:, PROBST:PROBST + 2, :].rearrange("p a (b t) -> p (a b) t", t=P)

        AT = N + 1
        STEPS = range(-1, AT + N + 3)
        UNITS = [(kind, h, i) for h in range(HALVES) for kind in ("ctx", "keys", "values") for i in range(2)]
        FILL_A = {-1: 0, 0: 1, 1: 3, 2: 5, 3: 6, 4: 8, 5: 9, 6: 10, 7: 11}
        FILL_B = {0: 2, 1: 4, 3: 7}
        QUERIES = {7: 0, 11: 1}
        WARM_UP = 6
        SPLIT = {1: 0, 2: 1, 4: 2, 6: 3}
        MLP = {AT + 7: [("fc", 0), ("fc", 1)], AT + 7.3: [("fc", 2), ("fc", 3)], AT + 8: [("fc", 4), ("fc", 5)],
               AT + 8.3: [("fc", 6), ("fc", 7)], AT + 9: [("pj", 0), ("pj", 1)], AT + 9.3: [],
               AT + 10: [("pj", 2), ("pj", 3)], AT + 10.3: []}

        def units(at, t):
            return [UNITS[at[t]]] if t in at else []

        block = ctx.enter_context(nc.Block())

        def load_vec(eng, layer, name, at, done):
            v = A[f"L{layer}_xattn_" + name]
            if layer == 0:
                dst = vec0_rows[at - L0_BV:at - L0_BV + 1, :].rearrange("r (e c) -> r e c", e=2)
                src = v.rearrange("(r o c) -> r o c", r=1, o=1).broadcast_to([1, 2, C])
            else:
                dst, src = vec_rows[at:at + v.shape[0] // P, :], v.rearrange("(r p) -> r p", p=P)
            eng.dma_start(dst, src).then_inc(done, 16)

        def load_twice(eng, name, w, done):
            src = A["L0_xattn_" + name].rearrange("(o c) m -> o c m", o=1).broadcast_to([2, C, C])
            eng.dma_start(w[:], src).then_inc(done, 16)

        def load_weight(eng, name, w, s):
            eng.dma_start(w[:], A["L1_xattn_" + name].rearrange("(g p) n -> p g n", p=P)).then_inc(w_loaded[s], 16)

        def load_pairs(eng, name, dst, sems, i):
            a, b = LOADS[i]
            eng.dma_start(dst[:, a:b, :], pairs(A[name], a, b)).then_inc(sems[i], 16)

        @block.sync
        def _(sp):
            load_twice(sp, "w_t", wt0, wt_loaded)
            load_twice(sp, "w_v", wv0, wv0_loaded)
            load_pairs(sp, "x", rows, x_loaded, 0)
            load_pairs(sp, "x", rows, x_loaded, 1)
            load_weight(sp, "k_w", wk, "k")
            for name, at in (("ln1_w", LN1_W), ("ln1_b", LN1_B), ("q_b", Q_B), ("k_b", K_B), ("v_b", V_B),
                             ("ln2_w", LN2_W), ("ln2_b", LN2_B), ("fc_b", FC_B)):
                load_vec(sp, 1, name, at, vec_loaded)
            load_weight(sp, "v_w", wv, "v")
            load_pairs(sp, "ctx_2048", ys, y_loaded, 2)
            load_pairs(sp, "x", rows, x_loaded, 2)
            load_weight(sp, "q_w", wq, "q")
            load_weight(sp, "cproj_w", wc, "c")
            fc = A["L1_xattn_fc_w"].rearrange("(g p) n -> g p n", p=P)
            pj = A["L1_xattn_proj_w"].rearrange("(a m p) n -> a p m n", p=P, m=W // D)
            for c in range(WPARTS):
                wait(sp, "part_lo", c)
                if c < G:
                    sp.dma_start(wstage[:], fc[c]).then_inc(w_loaded["part"], 16)
                else:
                    sp.dma_start(wstage[:].rearrange("p (m n) -> p m n", n=D), pj[c - G]
                                 ).then_inc(w_loaded["part"], 16)
            for n in range(N):
                wait(sp, "out_ready", n + 1)
                sp.dma_start(pairs(out, n, n + 1), rows[:, n:n + 1, :]).then_inc(stored, 16)
            sp.wait_ge(stored, N * 16)

        @block.gpsimd
        def _(pool):
            pool.memset(ones[:], 1.0).then_inc(ones_ready, 1)
            pool.wait_ge(ones_ready, 1)
            pool.affine_select(out=ident[:], in_=ones[:], compare_op=ALU.is_equal, fill=0.0, base=0,
                               pattern=[[-1, P]], channel_multiplier=1).then_inc(ident_ready, 1)
            load_vec(pool, 0, "b_v", L0_BV, vec0_loaded)
            load_vec(pool, 0, "b_t", L0_BT, vec0_loaded)
            pool.memset(half_power[:], -0.5).then_inc(zeros_ready, 1)
            pool.memset(uext[:], 1.0).then_inc(zeros_ready, 1)
            pool.memset(vals[:], 0.0).then_inc(zeros_ready, 1)
            for e in range(2):
                src = A["mask_BxS2_bf1"].rearrange("(n e) k -> e n k", e=2)[e:e + 1].broadcast_to([C, N, C])
                pool.dma_start(mask8[e * C:(e + 1) * C, :, :], src).then_inc(w_loaded["mask"], 16)
            pool.wait_ge(zeros_ready, 3)

            def inverse_std(name, n, meanvar):
                wait(pool, name + "_meanvar", n + 1)
                pool.tensor_scalar(vareps[:], meanvar[:, n % 2, 1:2], LN_EPS, 1.0, ALU.add,
                                   ALU.mult).then_inc(S[name + "_vareps"], 1)
                wait(pool, name + "_vareps", n + 1)
                pool.tensor_tensor(rstd[:], vareps[:], half_power[:], ALU.pow).then_inc(S[name + "_rstd"], 1)
                wait(pool, name + "_rstd", n + 1)

            for t in STEPS:
                n = t - 2
                if 0 <= n < N:
                    wait(pool, "relu_out", n + 1)
                    pool.tensor_tensor(rows[:, n, :], rows[:, n, :], rout[:], ALU.add).then_inc(S["x1_ready"], 1)
                n = t
                if 0 <= n < N:
                    for e in range(2):
                        wait(pool, "rowsum_inv", 2 * n + e + 1)
                        wait(pool, "mixed", 2 * (n - 2) + e + 1)
                        for j in range(2):
                            pool.tensor_scalar(us[:, n % 2, e, j, :], uext[:, n % 2, j, e * C:e * C + P],
                                               rinv[:, n % 2, e, j:j + 1], 1.0, ALU.mult,
                                               ALU.mult).then_inc(S["scaled_u"], 1)
                if t == 0:
                    for name, w, s in (("cproj_b", cproj_b, "cb"), ("proj_b", proj_b, "pb")):
                        src = A["L1_xattn_" + name].rearrange("(o d) -> o d", o=1).broadcast_to([P, D])
                        pool.dma_start(w[:], src).then_inc(w_loaded[s], 16)
                n = t - 2
                if 0 <= n < N:
                    inverse_std("x1", n, mv)
                    wait(pool, "x1_turned", n - 1)
                    pool.tensor_scalar(xn[:, n % 2, :], rows[:, n, :], mv[:, n % 2, 0:1], rstd[:, 0:1], ALU.subtract,
                                       ALU.mult).then_inc(S["x1_normed"], 1)
                    if n == 0:
                        pool.wait_ge(w_loaded["cb"], 16)
                        pool.wait_ge(w_loaded["pb"], 16)
                    wait(pool, "x1_normed", n + 1)
                    pool.tensor_tensor(rows[:, n, :], rows[:, n, :], cproj_b[:], ALU.add).then_inc(S["x1_plus_bias"], 1)
                if t in SPLIT:
                    c = SPLIT[t]
                    wait(pool, "part_hi", c + 1)
                    hi, lo = (wfc, wpj)[c // G]
                    k = c % G
                    hi, lo = (x[:, k, :] if c < G else x[:, k * (W // D):(k + 1) * (W // D), :] for x in (hi, lo))
                    src = wstage[:] if c < G else wstage[:].rearrange("p (m n) -> p m n", n=D)
                    pool.tensor_tensor(lo, src, hi.bitcast(F32), ALU.subtract).then_inc(S["part_lo"], 1)

                n = t - AT - 2
                if 0 <= n < N:
                    inverse_std("hid", n, mv)
                    wait(pool, "hid_turned", n - 1)
                    pool.tensor_scalar(hn[:, n % 2, :], rows[:, n, :], mv[:, n % 2, 0:1], rstd[:, 0:1], ALU.subtract,
                                       ALU.mult).then_inc(S["hid_normed"], 1)
                    wait(pool, "hid_normed", n + 1)
                    pool.tensor_tensor(rows[:, n, :], rows[:, n, :], proj_b[:], ALU.add).then_inc(S["hid_plus_bias"], 1)
                n = t - AT - 3
                if 0 <= n < N:
                    wait(pool, "hid_hi", n + 1)
                    cols = slice(n * P, (n + 1) * P)
                    pool.tensor_tensor(hidT[1][:, :, cols], hidf[:], hidT[0][:, :, cols].bitcast(F32),
                                       ALU.subtract).then_inc(S["hid_lo"], 1)
                n = t - AT + 1
                if 0 <= n < N:
                    wait(pool, "probs_inv", n + 1)
                    heads = probs[:, n % 2, :].rearrange("p (h k) -> p h k", h=H)
                    pool.tensor_tensor(heads, heads, pinv[:, n % 2, :].unsqueeze(2).broadcast_to([P, H, C]),
                                       ALU.mult).then_inc(S["probs_ready"], 1)

        def gelu(act, h, unit):
            k = M * h + unit[1]
            wait(act, "fc_made", k + 1)
            wait(act, "ff_lo", k - 1)
            act.activation(act_ff[:, k % 2, :], bank(k % 4), ACT.Gelu_apprx_tanh,
                           bias=col(FC_B + unit[1])).then_inc(S["gelu_ready"], 1)

        @block.scalar
        def _(act):
            load_twice(act, "w_qk", wqk, wqk_loaded)
            load_pairs(act, "ctx_2048", ys, y_loaded, 0)
            load_pairs(act, "ctx_2048", ys, y_loaded, 1)

            def identity(dst, src, bias, scale, done):
                act.activation(dst, src, ACT.Identity, bias=bias, scale=scale).then_inc(S[done], 1)

            def fill(unit):
                kind, h, i = unit
                if kind == "ctx":
                    wait(act, "ctx_turned", 2 * h + i + 1)
                    wait(act, "values_made", 2 * h)
                    act.copy(ctxT[:, :, 2 * i * P:2 * (i + 1) * P].rearrange("p g (a t) -> p a g t", a=2),
                             bank(FILL).rearrange("p (a g t) -> p a g t", a=2, g=G)).then_inc(S["ctx_ready"], 1)
                if kind == "values":
                    wait(act, "values_made", 2 * h + i + 1)
                    if h == i == 0:
                        act.wait_ge(zeros_ready, 3)
                    for a in range(2):
                        n = NH * h + 2 * i + a
                        for e in range(2):
                            src = psum[e * C:(e + 1) * C, FILL, a * D:(a + 1) * D].rearrange(
                                "p (i b d) -> p i b d", b=2, d=HD)
                            for b in range(2):
                                act.copy(vals[b * C:(b + 1) * C, n, e, :, b * HD:(b + 1) * HD],
                                         src[:, :, b, :]).then_inc(S["values_ready"], 1)

            def energy_exp(n, e):
                wait(act, "energy_max", 2 * n + e + 1)
                wait(act, "mixed", 2 * (n - 2) + e + 1)
                for j in range(2):
                    act.activation(att[:, n % 2, e, j, :], halfbank(ENERGY + e, j), ACT.Exp,
                                   bias=nmax[:, n % 2, e, j:j + 1],
                                   accum_out=rsum[:, n % 2, e, j:j + 1]).then_inc(S["energy_exp"], 1)

            act.add_instruction(mybir.InstLoadActFuncSet(name=nc.get_next_instruction_name(),
                                                         act_func_set_id=EXP_LN_SET, ins=[], outs=[]))
            for t in STEPS:
                if 0 <= t < N:
                    energy_exp(t, 0)
                n = t - 2
                if 0 <= n < N:
                    wait(act, "relu_in", n + 1)
                    wait(act, "x1_ready", n)
                    if n == 0:
                        act.wait_ge(vec0_ready, 1)
                    act.activation(rout[:], rin[:, n % 2, :], ACT.Relu, bias=col(L0_BT)).then_inc(S["relu_out"], 1)
                if 0 <= t < N:
                    energy_exp(t, 1)
                for u in units(FILL_A, t):
                    fill(u)
                n = t - 1
                if 0 <= n < N:
                    wait(act, "wtx_made", n + 1)
                    for e in range(2):
                        act.activation(csln[e * C:(e + 1) * C, :],
                                       psum[(1 - e) * C:(2 - e) * C, MIX + n % 2, e * D:(e + 1) * D], ACT.Ln,
                                       bias=COLSUM_EPS).then_inc(S["colsum_ln"], 1)
                    wait(act, "colsum_ln", 2 * n + 2)
                    wait(act, "mix_normed", 2 * n)
                    act.activation(csinv[:], csln[:], ACT.Exp, scale=-1.0).then_inc(S["colsum_inv"], 1)
                for u in units(FILL_B, t):
                    fill(u)
                if t in QUERIES:
                    for g in range(G):
                        wait(act, "queries_made", G * QUERIES[t] + g + 1)
                        identity(queries[:, g, QUERIES[t] * TOK:(QUERIES[t] + 1) * TOK], bank(FILL), col(Q_B + g), 1.0,
                                 "queries_ready")
                n = t - 3
                if 0 <= n < N:
                    wait(act, "x1_turned", n + 1)
                    wait(act, "queries_made", G * (n // NH))
                    if n == 0:
                        act.wait_ge(vec_ready, 1)
                    for g in range(G):
                        identity(x1T[:, g, (n % NH) * P:(n % NH + 1) * P], psum[:, TURN, g * P:(g + 1) * P],
                                 col(LN1_B + g), col(LN1_W + g), "x1t_ready")

                n = t - AT - 3
                if 0 <= n < N:
                    wait(act, "hid_turned", n + 1)
                    wait(act, "hid_lo", n)
                    for g in range(G):
                        identity(hidf[:, g, :], psum[:, FILL, g * P:(g + 1) * P], col(LN2_B + g), col(LN2_W + g),
                                 "hidf_ready")
                for u in MLP.get(t, []):
                    gelu(act, 0, u) if u[0] == "fc" else None
                n = t - AT - 1
                if 0 <= n < N:
                    wait(act, "heads_made", n + 1)
                    for g in range(G):
                        identity(hdT[:, g, :], psum[:, HEADS, g * P:(g + 1) * P], col(V_B + g), 1.0, "heads_ready")
                for u in MLP.get(t + 0.3, []):
                    gelu(act, 0, u) if u[0] == "fc" else None
                n = t - AT + 1
                if 0 <= n < N:
                    wait(act, "scores_shifted", n + 1)
                    act.activation(probs[:, n % 2, :], probs[:, n % 2, :], ACT.Exp,
                                   scale=SCALE).then_inc(S["probs_exp"], 1)
                n = t - AT
                if 0 <= n < N:
                    wait(act, "probs_turned", n + 1)
                    act.copy(prT[:, 0:HP // 2, :].rearrange("p a t -> p (a t)"), bank(PROBST)
                             ).then_inc(S["probst_ready"], 1)
            for m in range(M):
                gelu(act, 1, ("fc", m))

        @block.vector
        def _(dve):
            for w in (wtT, gram, wtvT):
                ins = dve.memset(w[:], 0.0)
            ins.then_inc(diag_zeroed, 1)
            dve.wait_ge(ident_ready, 1)
            dve.tensor_reduce(parity[:], ident[:].rearrange("p (j a d) -> p a j d", a=2, d=HD), AX.XY,
                              ALU.add).then_inc(parity_ready, 1)
            dve.wait_ge(diag_zeroed, 1)

            def diagonal(dst, b, done):
                for e in range(2):
                    r = slice(e * C, (e + 1) * C)
                    dve.tensor_copy(dst[r, r], psum[r, b, 0:C]).then_inc(done, 1)

            dve.wait_ge(wt_turned, 1)
            diagonal(wtT, SETUP_WT, wt_ready)
            dve.wait_ge(gram_made, 1)
            diagonal(gram, SETUP_GRAM, gram_ready)
            dve.wait_ge(vec0_turned, 1)
            dve.tensor_copy(vec[:, L0_BV:VEC_ROWS], psum[:, SETUP_VEC0, 0:VEC_ROWS - L0_BV]).then_inc(vec0_ready, 1)
            dve.wait_ge(wtv_made, 1)
            diagonal(wtvT, SETUP_WTV, wtv_ready)
            dve.wait_ge(vec0_ready, 1)
            dve.tensor_scalar(bv_cols[:], ones[:], col(L0_BV), None, ALU.mult).then_inc(bv_ready, 1)

            def fill(unit):
                kind, h, g = unit
                if kind == "keys":
                    if h == g == 0:
                        dve.wait_ge(parity_ready, 1)
                        dve.wait_ge(vec_turned, 1)
                        dve.tensor_copy(vec[:, 0:L0_BV], psum[:, SETUP_VEC, 0:L0_BV]).then_inc(vec_ready, 1)
                        dve.wait_ge(vec_ready, 1)
                    wait(dve, "keys_made", 2 * h + g + 1)
                    for a in range(2):
                        dve.tensor_scalar(keys[:, g, a, h * TOK:(h + 1) * TOK], bank(FILL), col(K_B + g),
                                          parity[:, a:a + 1], ALU.add, ALU.mult).then_inc(S["keys_ready"], 1)

            def mean_var(name, n):
                dve.bn_stats(stats[:], rows[:, n, :]).then_inc(S[name + "_stats"], 1)
                wait(dve, name + "_stats", n + 1)
                dve.bn_aggr(mv[:, n % 2, :], stats[:]).then_inc(S[name + "_meanvar"], 1)

            def split_ff(h, m):
                k = M * h + m
                wait(dve, "gelu_ready", k + 1)
                wait(dve, "mlp_made", NH * h)
                dve.tensor_copy(ff[0][:, m, :], act_ff[:, k % 2, :]).then_inc(S["ff_hi"], 1)
                wait(dve, "ff_hi", k + 1)
                dve.tensor_tensor(ff[1][:, m, :], act_ff[:, k % 2, :], ff[0][:, m, :].bitcast(F32),
                                  ALU.subtract).then_inc(S["ff_lo"], 1)

            def result(h, i):
                n = NH * h + i
                wait(dve, "mlp_made", n + 1)
                wait(dve, "hid_plus_bias", n + 1)
                dve.tensor_tensor(rows[:, n, :], halfbank(MLP_BANKS[i], 0), rows[:, n, :],
                                  ALU.add).then_inc(S["out_ready"], 1)

            def mlp_unit(h, unit):
                (split_ff if unit[0] == "fc" else result)(h, unit[1])

            for t in STEPS:
                n = t
                if 0 <= n < N:
                    for e in range(2):
                        wait(dve, "energy_made", 2 * n + e + 1)
                        wait(dve, "energy_exp", 2 * (2 * (n - 2) + e + 1))
                        dve.tensor_reduce(nmax[:, n % 2, e, :], bank(ENERGY + e).rearrange("p (j m) -> p j m", j=2),
                                          AX.X, ALU.max, negate=True).then_inc(S["energy_max"], 1)
                n = t + 1
                if 0 <= n < N:
                    wait(dve, "proj_made", n + 1)
                    dve.tensor_copy(gx[:, n % 2, :], halfbank(PROJ0, 0)).then_inc(S["proj_ready"], 1)
                    wait(dve, "scaled_u", 4 * (n - 1))
                    if n == 0:
                        dve.wait_ge(wtbv_made, 1)
                        dve.tensor_copy(wtbv[:], psum[:, SETUP_WTBV, 0:P]).then_inc(wtbv_ready, 1)
                        dve.wait_ge(wtbv_ready, 1)
                        dve.wait_ge(zeros_ready, 3)
                    dst = uext[:, n % 2, :, :].rearrange("p j (b c) -> p j b c", b=3)[:, :, 0:3:2, :]
                    dve.tensor_tensor(dst, halfbank(PROJ0, 1).rearrange("p (j b c) -> p j b c", j=2, b=2),
                                      wtbv[:].rearrange("p (b c) -> p b c", b=2).unsqueeze(1)
                                      .broadcast_to([P, 2, 2, C]), ALU.add).then_inc(S["proj_ready"], 1)
                n = t
                if 0 <= n < N:
                    for e in range(2):
                        wait(dve, "energy_exp", 2 * (2 * n + e + 1))
                        wait(dve, "scaled_u", 4 * (n - 1))
                        dve.reciprocal(rinv[:, n % 2, e, :], rsum[:, n % 2, e, :]).then_inc(S["rowsum_inv"], 1)
                for u in units(FILL_A, t):
                    fill(u)
                n = t - 2
                if 0 <= n < N:
                    wait(dve, "x1_ready", n + 1)
                    mean_var("x1", n)
                if t in SPLIT:
                    c = SPLIT[t]
                    dve.wait_ge(w_loaded["part"], 16 * (c + 1))
                    k = c % G
                    hi = wfc[0][:, k, :] if c < G else wpj[0][:, k * (W // D):(k + 1) * (W // D), :]
                    src = wstage[:] if c < G else wstage[:].rearrange("p (m n) -> p m n", n=D)
                    dve.tensor_copy(hi, src).then_inc(S["part_hi"], 1)
                for u in units(FILL_B, t):
                    fill(u)
                if t == 5:
                    dve.wait_ge(w_loaded["mask"], 32)
                    dve.tensor_scalar(maskadd[:], mask8[:], -1.0, -FLOAT_MIN, ALU.add,
                                      ALU.mult).then_inc(mask_ready, 1)
                n = t - 1
                if 0 <= n < N:
                    wait(dve, "colsum_inv", n + 1)
                    for e in range(2):
                        dve.tensor_tensor(mixn[e * C:(e + 1) * C, :],
                                          psum[e * C:(e + 1) * C, MIX + n % 2, e * D:(e + 1) * D],
                                          csinv[e * C:(e + 1) * C, :], ALU.mult).then_inc(S["mix_normed"], 1)
                    wait(dve, "mix_normed", 2 * n + 2)
                    wait(dve, "relu_out", n - 1)
                    dve.tensor_tensor(rin[:, n % 2, :], halfbank(WTX, 0), mixn[:],
                                      ALU.subtract).then_inc(S["relu_in"], 1)

                n = t - AT - 2
                if 0 <= n < N:
                    wait(dve, "attn_made", n + 1)
                    wait(dve, "x1_plus_bias", n + 1)
                    dve.tensor_tensor(rows[:, n, :], halfbank(HEADS, 0), rows[:, n, :],
                                      ALU.add).then_inc(S["hidden_ready"], 1)
                    wait(dve, "hidden_ready", n + 1)
                    mean_var("hid", n)
                n = t - AT - 3
                if 0 <= n < N:
                    wait(dve, "hidf_ready", 2 * n + 2)
                    dve.tensor_copy(hidT[0][:, :, n * P:(n + 1) * P], hidf[:]).then_inc(S["hid_hi"], 1)
                for u in MLP.get(t, []):
                    mlp_unit(0, u)
                n = t - AT + 1
                s = n % 2
                if 0 <= n < N:
                    def heads():
                        return probs[:, s, :].rearrange("p (h k) -> p h k", h=H)

                    wait(dve, "scores_made", n + 1)
                    if n == 0:
                        dve.wait_ge(mask_ready, 1)
                    wait(dve, "probs_turned", n - 1)
                    dve.tensor_tensor(probs[:, s, :].rearrange("p (j i k) -> p j i k", j=J, k=C),
                                      scores_ps.rearrange("p j (i k) -> p j i k", k=C),
                                      maskadd[:, n:n + 1, :].unsqueeze(1).broadcast_to([P, J, H // J, C]),
                                      ALU.add).then_inc(S["scores_masked"], 1)
                    wait(dve, "scores_masked", n + 1)
                    dve.tensor_reduce(smax[:], heads(), AX.X, ALU.max).then_inc(S["scores_max"], 1)
                    wait(dve, "scores_max", n + 1)
                    dve.tensor_tensor(heads(), heads(), smax[:].unsqueeze(2).broadcast_to([P, H, C]),
                                      ALU.subtract).then_inc(S["scores_shifted"], 1)
                    wait(dve, "probs_exp", n + 1)
                    dve.tensor_reduce(psums[:, s, :], heads(), AX.X, ALU.add).then_inc(S["probs_sum"], 1)
                    wait(dve, "probs_sum", n + 1)
                    wait(dve, "probs_ready", n - 1)
                    dve.reciprocal(pinv[:, s, :], psums[:, s, :]).then_inc(S["probs_inv"], 1)
                for u in MLP.get(t + 0.3, []):
                    mlp_unit(0, u)
                n = t - AT
                if 0 <= n < N:
                    wait(dve, "probs_turned", n + 1)
                    dve.tensor_copy(prT[:, HP // 2:HP, :].rearrange("p a t -> p (a t)"), bank(PROBST + 1)
                                    ).then_inc(S["probst_ready"], 1)
            for m in range(M):
                mlp_unit(1, ("fc", m))
            for i in range(NH):
                mlp_unit(1, ("pj", i))

        @block.tensor
        def _(pe):
            def mm(dst, lhsT, rhs, start=True, stop=True):
                return pe.matmul(dst, lhsT, rhs, start=start, stop=stop)

            pe.wait_ge(ones_ready, 1)
            for _ in range(WARM_UP):
                mm(psum[:, ENERGY, 0:P], ones[:], ones[:])
            pe.wait_ge(ident_ready, 1)
            pe.wait_ge(wt_loaded, 16)
            for r in (slice(0, C), slice(C, P)):
                ins = mm(psum[r, SETUP_WT, 0:C], wt0[r, :], ident[r, r])
            ins.then_inc(wt_turned, 1)
            pe.wait_ge(wqk_loaded, 16)
            for r in (slice(0, C), slice(C, P)):
                ins = mm(psum[r, SETUP_GRAM, 0:C], wqk[r, :], wqk[r, :])
            ins.then_inc(gram_made, 1)
            pe.wait_ge(vec0_loaded, 2 * 16)
            pe.transpose(psum[:, SETUP_VEC0, 0:VEC_ROWS - L0_BV], vec0_rows[:],
                         ident[0:VEC_ROWS - L0_BV, 0:VEC_ROWS - L0_BV]).then_inc(vec0_turned, 1)
            pe.wait_ge(wv0_loaded, 16)
            pe.wait_ge(wt_ready, 2)
            for r in (slice(0, C), slice(C, P)):
                ins = mm(psum[r, SETUP_WTV, 0:C], wv0[r, :], wtT[r, r])
            ins.then_inc(wtv_made, 1)

            def free_fill(i):
                if i > 0:
                    kind, h, k = UNITS[i - 1]
                    wait(pe, *{"ctx": ("ctx_ready", 2 * h + k + 1), "keys": ("keys_ready", 2 * (2 * h + k + 1)),
                               "values": ("values_ready", 8 * (2 * h + k + 1))}[kind])

            def fill(i):
                kind, h, k = UNITS[i]
                free_fill(i)
                if kind == "ctx":
                    for a in range(2):
                        n = NH * h + 2 * k + a
                        landed(pe, y_loaded, n)
                        for g in range(G):
                            ins = pe.transpose(psum[:, FILL, a * D + g * P:a * D + (g + 1) * P],
                                               ys[:, n, g * P:(g + 1) * P], ident[:])
                    ins.then_inc(S["ctx_turned"], 1)
                if kind == "keys":
                    pe.wait_ge(w_loaded["k"], 16)
                    wait(pe, "ctx_ready", 2 * (h + 1))
                    for c in range(G):
                        ins = mm(bank(FILL), wk[:, c, k * P:(k + 1) * P], ctxT[:, c, :], c == 0, c == G - 1)
                    ins.then_inc(S["keys_made"], 1)
                if kind == "values":
                    pe.wait_ge(w_loaded["v"], 16)
                    for a in range(2):
                        tok = slice((2 * k + a) * P, (2 * k + a + 1) * P)
                        for c in range(G):
                            ins = mm(halfbank(FILL, a), ctxT[:, c, tok], wv[:, c, :], c == 0, c == G - 1)
                    ins.then_inc(S["values_made"], 1)

            def mlp_unit(h, unit):
                kind, i = unit
                if kind == "fc":
                    k = M * h + i
                    if k < 4:
                        wait(pe, "scores_masked", N)
                    wait(pe, "gelu_ready", k - 3)
                    wait(pe, "hid_lo", NH * (h + 1))
                    if k == 0:
                        wait(pe, "part_lo", WPARTS)
                    for c in range(G):
                        for a, b in ((0, 0), (0, 1), (1, 0)):
                            ins = mm(bank(k % 4), wfc[a][:, c, i * P:(i + 1) * P],
                                     hidT[b][:, c, h * TOK:(h + 1) * TOK], c == 0 and a + b == 0,
                                     c == G - 1 and (a, b) == (1, 0))
                    ins.then_inc(S["fc_made"], 1)
                else:
                    b0 = MLP_BANKS[i]
                    wait(pe, "probst_ready", 2 * N)
                    wait(pe, "out_ready", NH * h + i - 1)
                    for m in range(M):
                        if i == 0:
                            wait(pe, "ff_lo", M * h + m + 1)
                        for a, b in ((0, 0), (0, 1), (1, 0)):
                            ins = mm(halfbank(b0, 0), ff[a][:, m, i * P:(i + 1) * P], wpj[b][:, m, :],
                                     m == 0 and a + b == 0, m == M - 1 and (a, b) == (1, 0))
                    ins.then_inc(S["mlp_made"], 1)

            for t in STEPS:
                n = t
                if 0 <= n < N:
                    for e in range(2):
                        wait(pe, "proj_ready", 2 * n + 1)
                        wait(pe, "energy_exp", 2 * (2 * (n - 1) + e + 1))
                        landed(pe, y_loaded, n)
                        r = slice(e * C, (e + 1) * C)
                        for j in range(2):
                            ins = mm(halfbank(ENERGY + e, j), ys[r, n, j * P:(j + 1) * P], gx[r, n % 2, :])
                        ins.then_inc(S["energy_made"], 1)
                n = t + 1
                if 0 <= n < N:
                    if n == 0:
                        pe.wait_ge(gram_ready, 2)
                    landed(pe, x_loaded, n)
                    wait(pe, "proj_ready", 2 * n)
                    mm(halfbank(PROJ0, 0), gram[:], rows[:, n, :])
                    if n == 0:
                        pe.wait_ge(wtv_ready, 2)
                    for j in range(2):
                        ins = mm(psum[:, PROJ0, D + j * P:D + (j + 1) * P], rows[:, n, j * P:(j + 1) * P], wtvT[:])
                    ins.then_inc(S["proj_made"], 1)
                    if n == 0:
                        pe.wait_ge(bv_ready, 1)
                        mm(psum[:, SETUP_WTBV, 0:P], bv_cols[:], wtT[:]).then_inc(wtbv_made, 1)
                if t == 0:
                    pe.wait_ge(vec_loaded, 8 * 16)
                    pe.transpose(psum[:, SETUP_VEC, 0:L0_BV], vec_rows[:],
                                 ident[0:L0_BV, 0:L0_BV]).then_inc(vec_turned, 1)
                if t in FILL_A:
                    fill(FILL_A[t])
                n = t - 1
                if 0 <= n < N:
                    for e in range(2):
                        wait(pe, "scaled_u", 2 * (2 * n + e + 1))
                        wait(pe, "mix_normed", 2 * (n - 1))
                        for j in range(2):
                            ins = mm(halfbank(MIX + n % 2, e), us[:, n % 2, e, j, :], att[:, n % 2, e, j, :], j == 0,
                                     j == 1)
                        ins.then_inc(S["mixed"], 1)
                    wait(pe, "relu_in", n)
                    mm(halfbank(WTX, 0), wtT[:], rows[:, n, :]).then_inc(S["wtx_made"], 1)
                if t in FILL_B:
                    fill(FILL_B[t])
                n = t - 3
                if 0 <= n < N:
                    wait(pe, "x1_normed", n + 1)
                    wait(pe, "x1t_ready", 2 * n)
                    for g in range(G):
                        ins = pe.transpose(psum[:, TURN, g * P:(g + 1) * P], xn[:, n % 2, g * P:(g + 1) * P], ident[:])
                    ins.then_inc(S["x1_turned"], 1)
                if t in QUERIES:
                    h = QUERIES[t]
                    if h == 0:
                        pe.wait_ge(w_loaded["q"], 16)
                    wait(pe, "values_ready", 8 * 4)
                    wait(pe, "x1t_ready", 2 * NH * (h + 1))
                    for g in range(G):
                        wait(pe, "queries_ready", G * h + g)
                        for c in range(G):
                            ins = mm(bank(FILL), wq[:, c, g * P:(g + 1) * P], x1T[:, c, :], c == 0, c == G - 1)
                        ins.then_inc(S["queries_made"], 1)

                n = t - AT - 3
                if 0 <= n < N:
                    wait(pe, "hid_normed", n + 1)
                    wait(pe, "queries_ready", 2 * G)
                    wait(pe, "hidf_ready", 2 * n)
                    for g in range(G):
                        ins = pe.transpose(psum[:, FILL, g * P:(g + 1) * P], hn[:, n % 2, g * P:(g + 1) * P], ident[:])
                    ins.then_inc(S["hid_turned"], 1)
                n = t - AT + 1
                if 0 <= n < N:
                    if n == 0:
                        wait(pe, "energy_exp", 4 * N)
                        wait(pe, "mix_normed", 2 * (N - 1))
                    wait(pe, "queries_ready", G * (n // NH + 1))
                    wait(pe, "keys_ready", 4 * (n // NH + 1))
                    wait(pe, "scores_masked", n)
                    for g in range(G):
                        for e in range(2):
                            k = slice(n * P + e * C, n * P + (e + 1) * C)
                            for j in range(J):
                                r = slice(32 * j, 32 * (j + 1))
                                ins = mm(scores_ps[e * C:(e + 1) * C, j, g * P:(g + 1) * P], queries[r, g, k],
                                         keys[r, g, :, k])
                    ins.then_inc(S["scores_made"], 1)
                for u in MLP.get(t, []):
                    mlp_unit(0, u)
                n = t - AT - 1
                if 0 <= n < N:
                    wait(pe, "probst_ready", 2 * (n + 1))
                    wait(pe, "values_ready", 8 * 4)
                    wait(pe, "x1t_ready", 2 * N)
                    wait(pe, "hidden_ready", n)
                    for e in range(2):
                        for g in range(G):
                            for j in range(J):
                                ins = mm(psum[32 * j:32 * (j + 1), HEADS, g * P + e * C:g * P + (e + 1) * C],
                                         vals[:, n, e, g * J + j, :], prT[:, j * G + g, e * C:(e + 1) * C])
                    ins.then_inc(S["heads_made"], 1)
                for u in MLP.get(t + 0.3, []):
                    mlp_unit(0, u)
                n = t - AT
                if 0 <= n < N:
                    if n == 0:
                        wait(pe, "relu_in", N)
                    wait(pe, "probs_ready", n + 1)
                    wait(pe, "probst_ready", 2 * n)
                    for i in range(HP):
                        ins = pe.transpose(probsT_ps[:, i, :], probs[:, n % 2, i * P:(i + 1) * P], ident[:])
                    ins.then_inc(S["probs_turned"], 1)
                n = t - AT - 1
                if 0 <= n < N:
                    if n == 0:
                        pe.wait_ge(w_loaded["c"], 16)
                    wait(pe, "heads_ready", 2 * (n + 1))
                    for c in range(G):
                        ins = mm(halfbank(HEADS, 0), hdT[:, c, :], wc[:, c, :], c == 0, c == G - 1)
                    ins.then_inc(S["attn_made"], 1)
            for m in range(M):
                mlp_unit(1, ("fc", m))
            for i in range(NH):
                mlp_unit(1, ("pj", i))


_OUT = ((16, 64, 256), "float32")


def kernel(**inputs):
    import numpy as _np
    import concourse.bacc as _bacc
    from concourse import mybir as _mybir
    from concourse.bass_utils import run_bass_kernel_spmd as _run

    nc = _bacc.Bacc("TRN2", target_bir_lowering=False, num_devices=1)
    arrays, aps = {}, {}
    for name, a in inputs.items():
        a = _np.ascontiguousarray(a)
        if a.dtype == _np.bool_:
            a = a.view(_np.uint8)
        arrays[f"in_{name}_dram"] = a
        aps[name] = nc.dram_tensor(f"in_{name}_dram", a.shape, _mybir.dt.from_np(a.dtype), kind="ExternalInput").ap()
    out = nc.dram_tensor("out_0_dram", _OUT[0], _mybir.dt.from_np(_np.dtype(_OUT[1])), kind="ExternalOutput").ap()
    xattn_two_layers(nc, aps, out)
    r = _run(nc, [arrays], core_ids=[0])
    return r.results[0]["out_0_dram"]
```

```python
from contextlib import ExitStack

import concourse.bass as bass
from concourse import mybir

F32 = mybir.dt.float32
F32R = mybir.dt.float32r
U8 = mybir.dt.uint8
ALU = mybir.AluOpType
ACT = mybir.ActivationFunctionType
AX = mybir.AxisListType

P = 128
BANK = 512
EXP_LN_SET = 6
FLOAT_MIN = -3.4028234663852886e38
LN_EPS = 1e-5
COLSUM_EPS = 1e-7

LN1_W, LN1_B, Q_B, K_B, V_B, LN2_W, LN2_B = range(0, 14, 2)
FC_B = 14
L0_BV, L0_BT = 22, 23
VEC_ROWS = 24


def xattn_two_layers(nc, A, out):
    B, C, D = A["x"].shape
    H = 16
    HD = D // H
    FF = A["L1_xattn_fc_w"].shape[1]
    N = B // 2
    HALVES = 2
    NH = N // HALVES
    TOK = NH * P
    G = D // P
    J = P // (2 * HD)
    HP = G * J
    M = FF // P
    SCALE = float(HD) ** -0.5
    W = BANK
    WPARTS = 2 * G * FF // W

    with ExitStack() as ctx:
        def sb(name, shape, dt=F32):
            return ctx.enter_context(nc.sbuf_tensor(name, shape, dt))

        def sem(name):
            return ctx.enter_context(nc.semaphore(name))

        wqk = sb("wqk", [P, C])
        wv0 = sb("wv0", [P, C])
        wt0 = sb("wt0", [P, C])
        gram = sb("gram", [P, P])
        wtT = sb("wtT", [P, P])
        wtvT = sb("wtvT", [P, P])
        bv_cols = sb("bv_cols", [P, P])
        wtbv = sb("wtbv", [P, P])
        ident = sb("ident", [P, P])
        ones = sb("ones", [P, P])
        vec0_rows = sb("vec0_rows", [VEC_ROWS - L0_BV, P])
        vec_rows = sb("vec_rows", [L0_BV, P])
        vec = sb("vec", [P, VEC_ROWS])
        parity = sb("parity", [P, 2])
        keys_b = sb("keys_b", [P, G, 2])
        half_power = sb("half_power", [P, 1])
        wq = sb("wq", [P, G, D])
        wk = sb("wk", [P, G, D])
        wv = sb("wv", [P, G, D])
        wc = sb("wc", [P, G, D])
        wstage = sb("wstage", [P, 2, W])
        wfc = [sb("wfc_hi", [P, G, FF], F32R), sb("wfc_lo", [P, G, FF], F32R)]
        wpj = [sb("wpj_hi", [P, M, D], F32R), sb("wpj_lo", [P, M, D], F32R)]
        cproj_b = sb("cproj_b", [P, D])
        proj_b = sb("proj_b", [P, D])
        mask8 = sb("mask8", [P, N, C], U8)
        maskadd = sb("maskadd", [P, N, C])

        rows = sb("rows", [P, N, D])
        ys = sb("ys", [P, N, D])
        ctxT = sb("ctxT", [P, G, TOK])
        keys = sb("keys", [P, G, 2, N * P])
        vals = sb("vals", [P, N, 2, HP, 2 * HD])
        gx = sb("gx", [P, 2, D])
        uext = sb("uext", [P, 2, 2, 3 * C])
        us = sb("us", [P, 2, 2, 2, P])
        att = sb("att", [P, 2, 2, 2, D])
        nmax = sb("nmax", [P, 2, 2, 2])
        rsum = sb("rsum", [P, 2, 2, 2])
        rinv = sb("rinv", [P, 2, 2, 2])
        csln = sb("csln", [P, D])
        csinv = sb("csinv", [P, D])
        mixn = sb("mixn", [P, D])
        rin = sb("rin", [P, 2, D])
        rout = sb("rout", [P, D])
        stats = sb("stats", [P, 6])
        mv = sb("mv", [P, 2, 2])
        vareps = sb("vareps", [P, 1])
        rstd = sb("rstd", [P, 2, 1])
        shift = sb("shift", [P, 2, 1])
        xn = sb("xn", [P, 2, D])
        x1T = sb("x1T", [P, G, TOK])
        queries = sb("queries", [P, G, N * P])
        probs = sb("probs", [P, 2, G * BANK])
        smax = sb("smax", [P, H])
        psums = sb("psums", [P, 2, H])
        pinv = sb("pinv", [P, 2, H])
        prT = sb("prT", [P, HP, P])
        hdT = sb("hdT", [P, G, P])
        hn = sb("hn", [P, 2, D])
        hidf = sb("hidf", [P, G, P])
        hidT = [sb("hidT_hi", [P, G, N * P], F32R), sb("hidT_lo", [P, G, N * P], F32R)]
        act_ff = ys[:, 0:4, :].rearrange("p (k a) d -> p k (a d)", k=2)
        ff = [sb("ff_hi", [P, M, TOK], F32R), sb("ff_lo", [P, M, TOK], F32R)]

        psum = ctx.enter_context(nc.psum_tensor("psum", [P, 8, BANK], F32))
        PROJ0, ENERGY, MIX, WTX, TURN, FILL = 0, 1, 3, 5, 6, 7
        MLP_BANKS = [4, 5, 4, 5]
        SETUP_WT, SETUP_GRAM, SETUP_WTV, SETUP_VEC0, SETUP_WTBV, SETUP_VEC = 6, 5, 3, 4, 4, 6
        PROBST, HEADS = 4, 6

        wt_loaded, wqk_loaded, wv0_loaded = sem("wt_loaded"), sem("wqk_loaded"), sem("wv0_loaded")
        vec0_loaded, vec_loaded = sem("vec0_loaded"), sem("vec_loaded")
        x_loaded = [sem(f"x_loaded{i}") for i in range(3)]
        y_loaded = [sem(f"y_loaded{i}") for i in range(3)]
        w_loaded = {k: sem("w_loaded_" + k) for k in ("k", "v", "q", "c", "cb", "pb", "mask")}
        part_loaded = [sem("part_loaded0"), sem("part_loaded1")]
        diag_zeroed, ones_ready, ident_ready, zeros_ready = map(sem, ("diag_zeroed", "ones_ready", "ident_ready",
                                                                      "zeros_ready"))
        vec0_turned, vec0_ready, vec_turned, vec_ready, wt_turned, wt_ready = map(sem, (
            "vec0_turned", "vec0_ready", "vec_turned", "vec_ready", "wt_turned", "wt_ready"))
        bv_ready, gram_made, gram_ready, wtv_made, wtv_ready, wtbv_made, wtbv_ready = map(sem, (
            "bv_ready", "gram_made", "gram_ready", "wtv_made", "wtv_ready", "wtbv_made", "wtbv_ready"))
        mask_ready, parity_ready, keys_b_ready, stored = map(sem, ("mask_ready", "parity_ready", "keys_b_ready",
                                                                   "stored"))
        S = {k: sem(k) for k in (
            "part_hi part_lo ctx_turned ctx_ready keys_made keys_ready values_made values_ready "
            "proj_made proj_ready energy_made energy_max energy_exp rowsum_inv scaled_u mixed wtx_made colsum_ln "
            "colsum_inv mix_normed relu_in relu_out x1_ready x1_stats x1_meanvar x1_vareps x1_rstd x1_normed x1_turned "
            "x1t_ready queries_made queries_ready x1_plus_bias scores_made scores_masked scores_max scores_shifted "
            "probs_exp probs_sum probs_inv probs_ready probs_turned probst_ready heads_made heads_ready attn_made "
            "hidden_ready hid_stats hid_meanvar hid_vareps hid_rstd hid_shift hid_normed hid_turned hidf_ready hid_hi hid_lo "
            "hid_plus_bias fc_made gelu_ready ff_hi ff_lo mlp_made out_ready").split()}

        def wait(eng, name, count):
            if count > 0:
                eng.wait_ge(S[name], count)

        def bank(n):
            return psum[:, n, :]

        def halfbank(n, k):
            return psum[:, n, k * D:(k + 1) * D]

        def col(i):
            return vec[:, i:i + 1]

        def pairs(t, a, b):
            return t[2 * a:2 * b].rearrange("(n e) c m -> (e c) n m", e=2)

        LOADS = [(0, 1), (1, NH), (NH, N)]

        def landed(eng, sems, n):
            for (a, b), s in zip(LOADS, sems):
                if a <= n < b:
                    eng.wait_ge(s, 16)

        def part(c):
            if c < WPARTS // 2:
                g, b = c * W // FF, c % (FF // W)
                return wstage[:, c % 2, :], wfc[0][:, g, b * W:(b + 1) * W], wfc[1][:, g, b * W:(b + 1) * W]
            m = (c - WPARTS // 2) * (W // D)
            return (wstage[:, c % 2, :].rearrange("p (m n) -> p m n", n=D), wpj[0][:, m:m + W // D, :],
                    wpj[1][:, m:m + W // D, :])

        scores_ps = psum[:, 0:J, 0:G * P]
        probsT_ps = psum[:, PROBST:PROBST + 2, :].rearrange("p a (b t) -> p (a b) t", t=P)

        AT = N + 1
        STEPS = range(-1, AT + N + 3)
        UNITS = [(kind, h, i) for h in range(HALVES) for kind in ("ctx", "keys", "values") for i in range(2)]
        FILL_E = {0: 1}
        FILL_A = {-1: 0, 1: 3, 2: 5, 4: 6, 6: 7, AT + 1: 10, AT + 2: 11}
        FILL_B = {0: 2, 1: 4, N: 8}
        FILL_C = {N: 9}
        UNITS_BEFORE = [8, 10]
        WARM_UP = 6
        SPLIT = {1: 0, 2: 1, 3: 2, 4: 3, 5: 4, 6: 5, 7: 6, AT + 5: 7}
        MLP = {AT + 6.6: [("fc", 0), ("fc", 1)], AT + 7: [("fc", 2)], AT + 7.3: [("fc", 3)],
               AT + 7.6: [("fc", 4), ("fc", 5)], AT + 8: [("fc", 6)], AT + 8.3: [("fc", 7)], AT + 8.6: [("pj", 0)],
               AT + 9: [("pj", 1)], AT + 10: [("pj", 2)], AT + 10.6: [("pj", 3)]}

        def queries_bank(h, g):
            return PROJ0 if (h, g) == (0, 1) else FILL

        def units(at, t):
            return [UNITS[at[t]]] if t in at else []

        block = ctx.enter_context(nc.Block())

        def load_vec(eng, layer, name, at, done):
            v = A[f"L{layer}_xattn_" + name]
            if layer == 0:
                dst = vec0_rows[at - L0_BV:at - L0_BV + 1, :].rearrange("r (e c) -> r e c", e=2)
                src = v.rearrange("(r o c) -> r o c", r=1, o=1).broadcast_to([1, 2, C])
            else:
                dst, src = vec_rows[at:at + v.shape[0] // P, :], v.rearrange("(r p) -> r p", p=P)
            eng.dma_start(dst, src).then_inc(done, 16)

        def load_twice(eng, name, w, done):
            src = A["L0_xattn_" + name].rearrange("(o c) m -> o c m", o=1).broadcast_to([2, C, C])
            eng.dma_start(w[:], src).then_inc(done, 16)

        def load_weight(eng, name, w, s):
            eng.dma_start(w[:], A["L1_xattn_" + name].rearrange("(g p) n -> p g n", p=P)).then_inc(w_loaded[s], 16)

        def load_pairs(eng, name, dst, sems, i):
            a, b = LOADS[i]
            eng.dma_start(dst[:, a:b, :], pairs(A[name], a, b)).then_inc(sems[i], 16)

        @block.sync
        def _(sp):
            load_twice(sp, "w_t", wt0, wt_loaded)
            load_twice(sp, "w_v", wv0, wv0_loaded)
            load_pairs(sp, "x", rows, x_loaded, 0)
            load_pairs(sp, "x", rows, x_loaded, 1)
            load_weight(sp, "k_w", wk, "k")
            for name, at in (("ln1_w", LN1_W), ("ln1_b", LN1_B), ("q_b", Q_B), ("k_b", K_B), ("v_b", V_B),
                             ("ln2_w", LN2_W), ("ln2_b", LN2_B), ("fc_b", FC_B)):
                load_vec(sp, 1, name, at, vec_loaded)
            load_weight(sp, "v_w", wv, "v")
            load_pairs(sp, "ctx_2048", ys, y_loaded, 2)
            load_pairs(sp, "x", rows, x_loaded, 2)
            load_weight(sp, "q_w", wq, "q")
            load_weight(sp, "cproj_w", wc, "c")
            fc = A["L1_xattn_fc_w"].rearrange("(g p) (b n) -> p g b n", p=P, n=W)
            pj = A["L1_xattn_proj_w"].rearrange("(m p) n -> p m n", p=P)
            for c in range(WPARTS):
                wait(sp, "part_lo", c - 1)
                if c < WPARTS // 2:
                    sp.dma_start(wstage[:, c % 2, :], fc[:, c * W // FF, c % (FF // W), :]).then_inc(part_loaded[c % 2], 16)
                else:
                    m = (c - WPARTS // 2) * (W // D)
                    sp.dma_start(wstage[:, c % 2, :].rearrange("p (m n) -> p m n", n=D),
                                 pj[:, m:m + W // D, :]).then_inc(part_loaded[c % 2], 16)
            for n in range(N):
                wait(sp, "out_ready", n + 1)
                sp.dma_start(pairs(out, n, n + 1), rows[:, n:n + 1, :]).then_inc(stored, 16)
            sp.wait_ge(stored, N * 16)

        @block.gpsimd
        def _(pool):
            pool.memset(ones[:], 1.0).then_inc(ones_ready, 1)
            pool.wait_ge(ones_ready, 1)
            pool.affine_select(out=ident[:], in_=ones[:], compare_op=ALU.is_equal, fill=0.0, base=0,
                               pattern=[[-1, P]], channel_multiplier=1).then_inc(ident_ready, 1)
            load_vec(pool, 0, "b_v", L0_BV, vec0_loaded)
            load_vec(pool, 0, "b_t", L0_BT, vec0_loaded)
            pool.memset(half_power[:], -0.5).then_inc(zeros_ready, 1)
            pool.memset(uext[:], 1.0).then_inc(zeros_ready, 1)
            pool.memset(vals[:], 0.0).then_inc(zeros_ready, 1)
            for e in range(2):
                src = A["mask_BxS2_bf1"].rearrange("(n e) k -> e n k", e=2)[e:e + 1].broadcast_to([C, N, C])
                pool.dma_start(mask8[e * C:(e + 1) * C, :, :], src).then_inc(w_loaded["mask"], 16)
            pool.wait_ge(zeros_ready, 3)

            def inverse_std(name, n):
                wait(pool, name + "_meanvar", n + 1)
                pool.tensor_scalar(vareps[:], mv[:, n % 2, 1:2], LN_EPS, 1.0, ALU.add,
                                   ALU.mult).then_inc(S[name + "_vareps"], 1)
                wait(pool, name + "_vareps", n + 1)
                wait(pool, name + "_normed", n - 1)
                pool.tensor_tensor(rstd[:, n % 2, :], vareps[:], half_power[:], ALU.pow).then_inc(S[name + "_rstd"], 1)

            def low_part(c):
                wait(pool, "part_hi", c + 1)
                src, hi, lo = part(c)
                pool.tensor_tensor(lo, src, hi.bitcast(F32), ALU.subtract).then_inc(S["part_lo"], 1)

            def residual(n):
                wait(pool, "relu_out", n + 1)
                pool.tensor_tensor(rows[:, n, :], rows[:, n, :], rout[:], ALU.add).then_inc(S["x1_ready"], 1)

            def first_norm(n):
                inverse_std("x1", n)
                if n == 0:
                    pool.wait_ge(w_loaded["cb"], 16)
                    pool.wait_ge(w_loaded["pb"], 16)
                wait(pool, "x1_normed", n + 1)
                pool.tensor_tensor(rows[:, n, :], rows[:, n, :], cproj_b[:], ALU.add).then_inc(S["x1_plus_bias"], 1)

            for t in STEPS:
                n = t
                if 0 <= n < N:
                    for e in range(2):
                        wait(pool, "rowsum_inv", 2 * n + e + 1)
                        wait(pool, "mixed", 2 * (n - 2) + e + 1)
                        for j in range(2):
                            pool.tensor_scalar(us[:, n % 2, e, j, :], uext[:, n % 2, j, e * C:e * C + P],
                                               rinv[:, n % 2, e, j:j + 1], 1.0, ALU.mult,
                                               ALU.mult).then_inc(S["scaled_u"], 1)
                if 0 <= t - 2 < N - 1:
                    residual(t - 2)
                if t == 0:
                    for name, w, s in (("cproj_b", cproj_b, "cb"), ("proj_b", proj_b, "pb")):
                        src = A["L1_xattn_" + name].rearrange("(o d) -> o d", o=1).broadcast_to([P, D])
                        pool.dma_start(w[:], src).then_inc(w_loaded[s], 16)
                if 0 <= t - 2 < N - 1:
                    first_norm(t - 2)
                if t == N:
                    residual(N - 1)
                    first_norm(N - 1)
                if 0 <= t < N and t in SPLIT:
                    low_part(SPLIT[t])

                n = t - AT - 3
                if 0 <= n < N:
                    wait(pool, "hid_hi", n + 1)
                    cols = slice(n * P, (n + 1) * P)
                    pool.tensor_tensor(hidT[1][:, :, cols], hidf[:], hidT[0][:, :, cols].bitcast(F32),
                                       ALU.subtract).then_inc(S["hid_lo"], 1)
                n = t - AT - 2
                if 0 <= n < N:
                    inverse_std("hid", n)
                    wait(pool, "hid_rstd", n + 1)
                    pool.tensor_scalar(shift[:, n % 2, :], mv[:, n % 2, 0:1], rstd[:, n % 2, :], -1.0, ALU.mult,
                                       ALU.mult).then_inc(S["hid_shift"], 1)
                n = t - AT + 1
                if 0 <= n < N:
                    wait(pool, "probs_inv", n + 1)
                    heads = probs[:, n % 2, :].rearrange("p (h k) -> p h k", h=H)
                    pool.tensor_tensor(heads, heads, pinv[:, n % 2, :].unsqueeze(2).broadcast_to([P, H, C]),
                                       ALU.mult).then_inc(S["probs_ready"], 1)
                n = t - AT - 2
                if 0 <= n < N:
                    wait(pool, "hid_normed", n + 1)
                    pool.tensor_tensor(rows[:, n, :], rows[:, n, :], proj_b[:], ALU.add).then_inc(S["hid_plus_bias"], 1)
                if t > N and t in SPLIT:
                    low_part(SPLIT[t])

        def gelu(act, h, unit):
            k = M * h + unit[1]
            wait(act, "fc_made", k + 1)
            wait(act, "ff_lo", k - 1)
            act.activation(act_ff[:, k % 2, :], bank(k % 4), ACT.Gelu_apprx_tanh,
                           bias=col(FC_B + unit[1])).then_inc(S["gelu_ready"], 1)

        @block.scalar
        def _(act):
            load_twice(act, "w_qk", wqk, wqk_loaded)
            load_pairs(act, "ctx_2048", ys, y_loaded, 0)
            load_pairs(act, "ctx_2048", ys, y_loaded, 1)

            def identity(dst, src, bias, scale, done):
                act.activation(dst, src, ACT.Identity, bias=bias, scale=scale).then_inc(S[done], 1)

            def fill(unit):
                kind, h, i = unit
                if kind == "ctx":
                    wait(act, "ctx_turned", 2 * h + i + 1)
                    wait(act, "values_made", 2 * h)
                    act.copy(ctxT[:, :, 2 * i * P:2 * (i + 1) * P].rearrange("p g (a t) -> p a g t", a=2),
                             bank(FILL).rearrange("p (a g t) -> p a g t", a=2, g=G)).then_inc(S["ctx_ready"], 1)
                if kind == "keys":
                    wait(act, "keys_made", 2 * h + i + 1)
                    if h == i == 0:
                        act.wait_ge(keys_b_ready, G)
                    for a in range(2):
                        identity(keys[:, i, a, h * TOK:(h + 1) * TOK], bank(FILL), keys_b[:, i, a:a + 1],
                                 parity[:, a:a + 1], "keys_ready")
                if kind == "values":
                    wait(act, "values_made", 2 * h + i + 1)
                    if h == i == 0:
                        act.wait_ge(zeros_ready, 3)
                    n = NH * h + 2 * i
                    for e in range(2):
                        src = psum[e * C:(e + 1) * C, FILL, :].rearrange("p (a i b d) -> p a i b d", a=2, b=2, d=HD)
                        for b in range(2):
                            act.copy(vals[b * C:(b + 1) * C, n:n + 2, e, :, b * HD:(b + 1) * HD],
                                     src[:, :, :, b, :]).then_inc(S["values_ready"], 1)

            def energy_exp(n, e):
                wait(act, "energy_max", 2 * n + e + 1)
                wait(act, "mixed", 2 * (n - 2) + e + 1)
                for j in range(2):
                    act.activation(att[:, n % 2, e, j, :], halfbank(ENERGY + e, j), ACT.Exp,
                                   bias=nmax[:, n % 2, e, j:j + 1],
                                   accum_out=rsum[:, n % 2, e, j:j + 1]).then_inc(S["energy_exp"], 1)

            act.add_instruction(mybir.InstLoadActFuncSet(name=nc.get_next_instruction_name(),
                                                         act_func_set_id=EXP_LN_SET, ins=[], outs=[]))
            def mlp_units(at):
                for u in MLP.get(at, []):
                    if u[0] == "fc":
                        gelu(act, 0, u)

            def relu(n):
                wait(act, "relu_in", n + 1)
                wait(act, "x1_ready", n)
                if n == 0:
                    act.wait_ge(vec0_ready, 1)
                act.activation(rout[:], rin[:, n % 2, :], ACT.Relu, bias=col(L0_BT)).then_inc(S["relu_out"], 1)

            def norm_weight(n):
                wait(act, "x1_turned", n + 1)
                wait(act, "queries_made", G * (n // NH))
                if n == 0:
                    act.wait_ge(vec_ready, 1)
                for g in range(G):
                    identity(x1T[:, g, (n % NH) * P:(n % NH + 1) * P], psum[:, TURN, g * P:(g + 1) * P],
                             col(LN1_B + g), col(LN1_W + g), "x1t_ready")

            def queries_bias(h, g):
                wait(act, "queries_made", G * h + g + 1)
                identity(queries[:, g, h * TOK:(h + 1) * TOK], bank(queries_bank(h, g)), col(Q_B + g), 1.0,
                         "queries_ready")

            for t in STEPS:
                for u in units(FILL_E, t):
                    fill(u)
                if 0 <= t < N:
                    energy_exp(t, 0)
                if 0 <= t - 2 < N - 1:
                    relu(t - 2)
                if 0 <= t < N:
                    energy_exp(t, 1)
                for u in units(FILL_A, t):
                    fill(u)
                n = t - 1
                if 0 <= n < N:
                    wait(act, "mixed", 2 * n + 2)
                    for e in range(2):
                        act.activation(csln[e * C:(e + 1) * C, :],
                                       psum[(1 - e) * C:(2 - e) * C, MIX + n % 2, e * D:(e + 1) * D], ACT.Ln,
                                       bias=COLSUM_EPS).then_inc(S["colsum_ln"], 1)
                    wait(act, "colsum_ln", 2 * n + 2)
                    wait(act, "mix_normed", 2 * n)
                    act.activation(csinv[:], csln[:], ACT.Exp, scale=-1.0).then_inc(S["colsum_inv"], 1)
                for u in units(FILL_B, t):
                    fill(u)
                if t == N - 1:
                    queries_bias(0, 0)
                if 0 <= t - 3 < N - 2:
                    norm_weight(t - 3)
                if t == N - 1:
                    queries_bias(0, 1)
                if t == N:
                    relu(N - 1)
                for u in units(FILL_C, t):
                    fill(u)
                if t == N:
                    norm_weight(N - 2)
                if t == AT:
                    norm_weight(N - 1)
                    queries_bias(1, 0)

                n = t - AT - 1
                if 0 <= n < N:
                    wait(act, "heads_made", n + 1)
                    for g in range(G):
                        identity(hdT[:, g, :], psum[:, HEADS, g * P:(g + 1) * P], col(V_B + g), 1.0, "heads_ready")
                mlp_units(t)
                n = t - AT - 3
                if 0 <= n < N:
                    wait(act, "hid_turned", n + 1)
                    wait(act, "hid_lo", n)
                    for g in range(G):
                        identity(hidf[:, g, :], psum[:, FILL, g * P:(g + 1) * P], col(LN2_B + g), col(LN2_W + g),
                                 "hidf_ready")
                    wait(act, "hidf_ready", 2 * n + 2)
                    act.copy(hidT[0][:, :, n * P:(n + 1) * P], hidf[:]).then_inc(S["hid_hi"], 1)
                n = t - AT + 1
                if 0 <= n < N:
                    wait(act, "scores_shifted", n + 1)
                    act.activation(probs[:, n % 2, :], probs[:, n % 2, :], ACT.Exp,
                                   scale=SCALE).then_inc(S["probs_exp"], 1)
                mlp_units(t + 0.3)
                n = t - AT
                if 0 <= n < N:
                    wait(act, "probs_turned", n + 1)
                    for k in range(2):
                        half = prT[:, k * HP // 2:(k + 1) * HP // 2, :]
                        act.copy(half.rearrange("p a t -> p (a t)"), bank(PROBST + k)).then_inc(S["probst_ready"], 1)
                if t == AT:
                    queries_bias(1, 1)
                n = t - AT - 2
                if 0 <= n < N:
                    wait(act, "hid_shift", n + 1)
                    wait(act, "hid_turned", n - 1)
                    act.activation(hn[:, n % 2, :], rows[:, n, :], ACT.Identity, bias=shift[:, n % 2, :],
                                   scale=rstd[:, n % 2, :]).then_inc(S["hid_normed"], 1)
                mlp_units(t + 0.6)
            for m in range(M):
                gelu(act, 1, ("fc", m))

        @block.vector
        def _(dve):
            for w in (wtT, gram, wtvT):
                ins = dve.memset(w[:], 0.0)
            ins.then_inc(diag_zeroed, 1)
            dve.wait_ge(ident_ready, 1)
            dve.tensor_reduce(parity[:], ident[:].rearrange("p (j a d) -> p a j d", a=2, d=HD), AX.XY,
                              ALU.add).then_inc(parity_ready, 1)
            dve.wait_ge(diag_zeroed, 1)

            def diagonal(dst, b, done):
                for e in range(2):
                    r = slice(e * C, (e + 1) * C)
                    dve.tensor_copy(dst[r, r], psum[r, b, 0:C]).then_inc(done, 1)

            dve.wait_ge(wt_turned, 1)
            diagonal(wtT, SETUP_WT, wt_ready)
            dve.wait_ge(gram_made, 1)
            diagonal(gram, SETUP_GRAM, gram_ready)
            dve.wait_ge(vec0_turned, 1)
            dve.tensor_copy(vec[:, L0_BV:VEC_ROWS], psum[:, SETUP_VEC0, 0:VEC_ROWS - L0_BV]).then_inc(vec0_ready, 1)
            dve.wait_ge(wtv_made, 1)
            diagonal(wtvT, SETUP_WTV, wtv_ready)
            dve.wait_ge(vec0_ready, 1)
            dve.tensor_scalar(bv_cols[:], ones[:], col(L0_BV), None, ALU.mult).then_inc(bv_ready, 1)

            def mean_var(name, n):
                dve.bn_stats(stats[:], rows[:, n, :]).then_inc(S[name + "_stats"], 1)
                wait(dve, name + "_stats", n + 1)
                dve.bn_aggr(mv[:, n % 2, :], stats[:]).then_inc(S[name + "_meanvar"], 1)

            def high_part(c):
                dve.wait_ge(part_loaded[c % 2], 16 * (c // 2 + 1))
                src, hi, lo = part(c)
                dve.tensor_copy(hi, src).then_inc(S["part_hi"], 1)

            def x1_norm(n):
                wait(dve, "x1_rstd", n + 1)
                wait(dve, "x1_turned", n - 1)
                dve.tensor_scalar(xn[:, n % 2, :], rows[:, n, :], mv[:, n % 2, 0:1], rstd[:, n % 2, :], ALU.subtract,
                                  ALU.mult).then_inc(S["x1_normed"], 1)

            def hidden(n):
                wait(dve, "attn_made", n + 1)
                wait(dve, "x1_plus_bias", n + 1)
                dve.tensor_tensor(rows[:, n, :], halfbank(HEADS, 0), rows[:, n, :],
                                  ALU.add).then_inc(S["hidden_ready"], 1)

            def hidden_mean_var(n):
                wait(dve, "hidden_ready", n + 1)
                mean_var("hid", n)

            def split_ff(h, m):
                k = M * h + m
                wait(dve, "gelu_ready", k + 1)
                wait(dve, "mlp_made", NH * h)
                dve.tensor_copy(ff[0][:, m, :], act_ff[:, k % 2, :]).then_inc(S["ff_hi"], 1)
                wait(dve, "ff_hi", k + 1)
                dve.tensor_tensor(ff[1][:, m, :], act_ff[:, k % 2, :], ff[0][:, m, :].bitcast(F32),
                                  ALU.subtract).then_inc(S["ff_lo"], 1)

            def result(h, i):
                n = NH * h + i
                wait(dve, "mlp_made", n + 1)
                wait(dve, "hid_plus_bias", n + 1)
                dve.tensor_tensor(rows[:, n, :], halfbank(MLP_BANKS[i], 0), rows[:, n, :],
                                  ALU.add).then_inc(S["out_ready"], 1)

            def mlp_unit(h, unit):
                (split_ff if unit[0] == "fc" else result)(h, unit[1])

            for t in STEPS:
                n = t
                if 0 <= n < N:
                    for e in range(2):
                        wait(dve, "energy_made", 2 * n + e + 1)
                        wait(dve, "energy_exp", 2 * (2 * (n - 2) + e + 1))
                        dve.tensor_reduce(nmax[:, n % 2, e, :], bank(ENERGY + e).rearrange("p (j m) -> p j m", j=2),
                                          AX.X, ALU.max, negate=True).then_inc(S["energy_max"], 1)
                n = t + 1
                if 0 <= n < N:
                    wait(dve, "proj_made", n + 1)
                    dve.tensor_copy(gx[:, n % 2, :], halfbank(PROJ0, 0)).then_inc(S["proj_ready"], 1)
                    wait(dve, "scaled_u", 4 * (n - 1))
                    if n == 0:
                        dve.wait_ge(wtbv_made, 1)
                        dve.tensor_copy(wtbv[:], psum[:, SETUP_WTBV, 0:P]).then_inc(wtbv_ready, 1)
                        dve.wait_ge(wtbv_ready, 1)
                        dve.wait_ge(zeros_ready, 3)
                    dst = uext[:, n % 2, :, :].rearrange("p j (b c) -> p j b c", b=3)[:, :, 0:3:2, :]
                    dve.tensor_tensor(dst, halfbank(PROJ0, 1).rearrange("p (j b c) -> p j b c", j=2, b=2),
                                      wtbv[:].rearrange("p (b c) -> p b c", b=2).unsqueeze(1)
                                      .broadcast_to([P, 2, 2, C]), ALU.add).then_inc(S["proj_ready"], 1)
                if 0 <= t - 3 < N - 2:
                    x1_norm(t - 3)
                n = t
                if 0 <= n < N:
                    for e in range(2):
                        wait(dve, "energy_exp", 2 * (2 * n + e + 1))
                        wait(dve, "scaled_u", 4 * (n - 1))
                        dve.reciprocal(rinv[:, n % 2, e, :], rsum[:, n % 2, e, :]).then_inc(S["rowsum_inv"], 1)
                if t == 0:
                    dve.wait_ge(vec_turned, 1)
                    dve.tensor_copy(vec[:, 0:L0_BV], psum[:, SETUP_VEC, 0:L0_BV]).then_inc(vec_ready, 1)
                    dve.wait_ge(parity_ready, 1)
                    dve.wait_ge(vec_ready, 1)
                    for g in range(G):
                        dve.tensor_scalar(keys_b[:, g, :], parity[:], col(K_B + g), None,
                                          ALU.mult).then_inc(keys_b_ready, 1)
                if 0 <= t < N and t in SPLIT:
                    high_part(SPLIT[t])
                if t == 5:
                    dve.wait_ge(w_loaded["mask"], 32)
                    dve.tensor_scalar(maskadd[:], mask8[:], -1.0, -FLOAT_MIN, ALU.add,
                                      ALU.mult).then_inc(mask_ready, 1)
                n = t - 1
                if 0 <= n < N:
                    wait(dve, "colsum_inv", n + 1)
                    for e in range(2):
                        dve.tensor_tensor(mixn[e * C:(e + 1) * C, :],
                                          psum[e * C:(e + 1) * C, MIX + n % 2, e * D:(e + 1) * D],
                                          csinv[e * C:(e + 1) * C, :], ALU.mult).then_inc(S["mix_normed"], 1)
                    wait(dve, "mix_normed", 2 * n + 2)
                    wait(dve, "wtx_made", n + 1)
                    wait(dve, "relu_out", n - 1)
                    dve.tensor_tensor(rin[:, n % 2, :], halfbank(WTX, 0), mixn[:],
                                      ALU.subtract).then_inc(S["relu_in"], 1)
                n = t - 2
                if 0 <= n < N - 1:
                    wait(dve, "x1_ready", n + 1)
                    mean_var("x1", n)
                if t == N:
                    x1_norm(N - 2)

                n = t - AT + 1
                s = n % 2
                if 0 <= n < N:
                    def heads():
                        return probs[:, s, :].rearrange("p (h k) -> p h k", h=H)

                    wait(dve, "scores_made", n + 1)
                    if n == 0:
                        dve.wait_ge(mask_ready, 1)
                    wait(dve, "probs_turned", n - 1)
                    dve.tensor_tensor(probs[:, s, :].rearrange("p (j i k) -> p j i k", j=J, k=C),
                                      scores_ps.rearrange("p j (i k) -> p j i k", k=C),
                                      maskadd[:, n:n + 1, :].unsqueeze(1).broadcast_to([P, J, H // J, C]),
                                      ALU.add).then_inc(S["scores_masked"], 1)
                    wait(dve, "scores_masked", n + 1)
                    dve.tensor_reduce(smax[:], heads(), AX.X, ALU.max).then_inc(S["scores_max"], 1)
                    if t == N:
                        wait(dve, "x1_ready", N)
                        mean_var("x1", N - 1)
                    wait(dve, "scores_max", n + 1)
                    dve.tensor_tensor(heads(), heads(), smax[:].unsqueeze(2).broadcast_to([P, H, C]),
                                      ALU.subtract).then_inc(S["scores_shifted"], 1)
                    if t == N:
                        x1_norm(N - 1)
                if 0 <= t - AT - 2 < N:
                    hidden_mean_var(t - AT - 2)
                for u in MLP.get(t, []):
                    mlp_unit(0, u)
                n = t - AT + 1
                if 0 <= n < N:
                    wait(dve, "probs_exp", n + 1)
                    dve.tensor_reduce(psums[:, s, :], heads(), AX.X, ALU.add).then_inc(S["probs_sum"], 1)
                    wait(dve, "probs_sum", n + 1)
                    wait(dve, "probs_ready", n - 1)
                    dve.reciprocal(pinv[:, s, :], psums[:, s, :]).then_inc(S["probs_inv"], 1)
                for u in MLP.get(t + 0.3, []):
                    mlp_unit(0, u)
                if 0 <= t - AT - 1 < N:
                    hidden(t - AT - 1)
                if t > N and t in SPLIT:
                    high_part(SPLIT[t])
                for u in MLP.get(t + 0.6, []):
                    mlp_unit(0, u)
            for m in range(M):
                mlp_unit(1, ("fc", m))
            for i in range(NH):
                mlp_unit(1, ("pj", i))

        @block.tensor
        def _(pe):
            def mm(dst, lhsT, rhs, start=True, stop=True):
                return pe.matmul(dst, lhsT, rhs, start=start, stop=stop)

            pe.wait_ge(ones_ready, 1)
            for _ in range(WARM_UP):
                mm(psum[:, ENERGY, 0:P], ones[:], ones[:])
            pe.wait_ge(ident_ready, 1)
            pe.wait_ge(wt_loaded, 16)
            for r in (slice(0, C), slice(C, P)):
                ins = mm(psum[r, SETUP_WT, 0:C], wt0[r, :], ident[r, r])
            ins.then_inc(wt_turned, 1)
            pe.wait_ge(wqk_loaded, 16)
            for r in (slice(0, C), slice(C, P)):
                ins = mm(psum[r, SETUP_GRAM, 0:C], wqk[r, :], wqk[r, :])
            ins.then_inc(gram_made, 1)
            pe.wait_ge(vec0_loaded, 2 * 16)
            pe.transpose(psum[:, SETUP_VEC0, 0:VEC_ROWS - L0_BV], vec0_rows[:],
                         ident[0:VEC_ROWS - L0_BV, 0:VEC_ROWS - L0_BV]).then_inc(vec0_turned, 1)
            pe.wait_ge(wv0_loaded, 16)
            pe.wait_ge(wt_ready, 2)
            for r in (slice(0, C), slice(C, P)):
                ins = mm(psum[r, SETUP_WTV, 0:C], wv0[r, :], wtT[r, r])
            ins.then_inc(wtv_made, 1)

            def free_fill(i):
                if i > 0:
                    kind, h, k = UNITS[i - 1]
                    wait(pe, *{"ctx": ("ctx_ready", 2 * h + k + 1), "keys": ("keys_ready", 2 * (2 * h + k + 1)),
                               "values": ("values_ready", 4 * (2 * h + k + 1))}[kind])

            def fill(i):
                kind, h, k = UNITS[i]
                free_fill(i)
                if i in UNITS_BEFORE:
                    wait(pe, "queries_ready", G * (UNITS_BEFORE.index(i) + 1))
                if kind == "ctx":
                    for a in range(2):
                        n = NH * h + 2 * k + a
                        landed(pe, y_loaded, n)
                        for g in range(G):
                            ins = pe.transpose(psum[:, FILL, a * D + g * P:a * D + (g + 1) * P],
                                               ys[:, n, g * P:(g + 1) * P], ident[:])
                    ins.then_inc(S["ctx_turned"], 1)
                if kind == "keys":
                    pe.wait_ge(w_loaded["k"], 16)
                    wait(pe, "ctx_ready", 2 * (h + 1))
                    for c in range(G):
                        ins = mm(bank(FILL), wk[:, c, k * P:(k + 1) * P], ctxT[:, c, :], c == 0, c == G - 1)
                    ins.then_inc(S["keys_made"], 1)
                if kind == "values":
                    pe.wait_ge(w_loaded["v"], 16)
                    for a in range(2):
                        tok = slice((2 * k + a) * P, (2 * k + a + 1) * P)
                        for c in range(G):
                            ins = mm(halfbank(FILL, a), ctxT[:, c, tok], wv[:, c, :], c == 0, c == G - 1)
                    ins.then_inc(S["values_made"], 1)

            def mlp_unit(h, unit):
                kind, i = unit
                if kind == "fc":
                    k = M * h + i
                    if k < 4:
                        wait(pe, "scores_masked", N)
                    wait(pe, "gelu_ready", k - 3)
                    wait(pe, "hid_lo", NH * (h + 1))
                    if k == 0:
                        wait(pe, "part_lo", WPARTS)
                    for c in range(G):
                        for a, b in ((0, 0), (0, 1), (1, 0)):
                            ins = mm(bank(k % 4), wfc[a][:, c, i * P:(i + 1) * P],
                                     hidT[b][:, c, h * TOK:(h + 1) * TOK], c == 0 and a + b == 0,
                                     c == G - 1 and (a, b) == (1, 0))
                    ins.then_inc(S["fc_made"], 1)
                else:
                    b0 = MLP_BANKS[i]
                    wait(pe, "probst_ready", 2 * N)
                    wait(pe, "out_ready", NH * h + i - 1)
                    for m in range(M):
                        if i == 0:
                            wait(pe, "ff_lo", M * h + m + 1)
                        for a, b in ((0, 0), (0, 1), (1, 0)):
                            ins = mm(halfbank(b0, 0), ff[a][:, m, i * P:(i + 1) * P], wpj[b][:, m, :],
                                     m == 0 and a + b == 0, m == M - 1 and (a, b) == (1, 0))
                    ins.then_inc(S["mlp_made"], 1)

            def turn_x1(n):
                wait(pe, "x1_normed", n + 1)
                wait(pe, "x1t_ready", 2 * n)
                for g in range(G):
                    ins = pe.transpose(psum[:, TURN, g * P:(g + 1) * P], xn[:, n % 2, g * P:(g + 1) * P], ident[:])
                ins.then_inc(S["x1_turned"], 1)

            def make_queries(h, g):
                if h == 0:
                    pe.wait_ge(w_loaded["q"], 16)
                if g == 0:
                    free_fill(UNITS_BEFORE[h])
                wait(pe, "x1t_ready", 2 * NH * (h + 1))
                if (h, g) == (0, 1):
                    wait(pe, "proj_ready", 2 * N)
                else:
                    wait(pe, "queries_ready", G * h + g)
                for c in range(G):
                    ins = mm(bank(queries_bank(h, g)), wq[:, c, g * P:(g + 1) * P], x1T[:, c, :], c == 0, c == G - 1)
                ins.then_inc(S["queries_made"], 1)

            for t in STEPS:
                n = t
                if 0 <= n < N:
                    for e in range(2):
                        wait(pe, "proj_ready", 2 * n + 1)
                        wait(pe, "energy_exp", 2 * (2 * (n - 1) + e + 1))
                        landed(pe, y_loaded, n)
                        r = slice(e * C, (e + 1) * C)
                        for j in range(2):
                            ins = mm(halfbank(ENERGY + e, j), ys[r, n, j * P:(j + 1) * P], gx[r, n % 2, :])
                        ins.then_inc(S["energy_made"], 1)
                if t in FILL_E:
                    fill(FILL_E[t])
                n = t + 1
                if 0 <= n < N:
                    if n == 0:
                        pe.wait_ge(gram_ready, 2)
                    landed(pe, x_loaded, n)
                    wait(pe, "proj_ready", 2 * n)
                    mm(halfbank(PROJ0, 0), gram[:], rows[:, n, :])
                    if n == 0:
                        pe.wait_ge(wtv_ready, 2)
                    for j in range(2):
                        ins = mm(psum[:, PROJ0, D + j * P:D + (j + 1) * P], rows[:, n, j * P:(j + 1) * P], wtvT[:])
                    ins.then_inc(S["proj_made"], 1)
                    if n == 0:
                        pe.wait_ge(bv_ready, 1)
                        mm(psum[:, SETUP_WTBV, 0:P], bv_cols[:], wtT[:]).then_inc(wtbv_made, 1)
                if t == 0:
                    pe.wait_ge(vec_loaded, 8 * 16)
                    pe.transpose(psum[:, SETUP_VEC, 0:L0_BV], vec_rows[:],
                                 ident[0:L0_BV, 0:L0_BV]).then_inc(vec_turned, 1)
                if t in FILL_A:
                    fill(FILL_A[t])
                n = t - 1
                if 0 <= n < N:
                    for e in range(2):
                        wait(pe, "scaled_u", 2 * (2 * n + e + 1))
                        wait(pe, "mix_normed", 2 * (n - 1))
                        for j in range(2):
                            ins = mm(halfbank(MIX + n % 2, e), us[:, n % 2, e, j, :], att[:, n % 2, e, j, :], j == 0,
                                     j == 1)
                        ins.then_inc(S["mixed"], 1)
                    wait(pe, "relu_in", n)
                    mm(halfbank(WTX, 0), wtT[:], rows[:, n, :]).then_inc(S["wtx_made"], 1)
                if t in FILL_B:
                    fill(FILL_B[t])
                if t == N - 1:
                    make_queries(0, 0)
                if 0 <= t - 3 < N - 2:
                    turn_x1(t - 3)
                if t == N - 1:
                    make_queries(0, 1)

                n = t - AT + 1
                if 0 <= n < N:
                    if n == 0:
                        wait(pe, "energy_exp", 4 * N)
                        wait(pe, "mix_normed", 2 * (N - 1))
                    wait(pe, "queries_ready", G * (n // NH + 1))
                    wait(pe, "keys_ready", 4 * (n // NH + 1))
                    wait(pe, "scores_masked", n)
                    for g in range(G):
                        for e in range(2):
                            k = slice(n * P + e * C, n * P + (e + 1) * C)
                            for j in range(J):
                                r = slice(32 * j, 32 * (j + 1))
                                ins = mm(scores_ps[e * C:(e + 1) * C, j, g * P:(g + 1) * P], queries[r, g, k],
                                         keys[r, g, :, k])
                    ins.then_inc(S["scores_made"], 1)
                if t in FILL_C:
                    fill(FILL_C[t])
                if t == N:
                    turn_x1(N - 2)
                if t == AT:
                    turn_x1(N - 1)
                    make_queries(1, 0)
                n = t - AT - 1
                if 0 <= n < N:
                    wait(pe, "probst_ready", 2 * (n + 1))
                    wait(pe, "values_ready", 4 * (n // 2 + 1))
                    wait(pe, "x1t_ready", 2 * N)
                    wait(pe, "hidden_ready", n)
                    for e in range(2):
                        for g in range(G):
                            for j in range(J):
                                ins = mm(psum[32 * j:32 * (j + 1), HEADS, g * P + e * C:g * P + (e + 1) * C],
                                         vals[:, n, e, g * J + j, :], prT[:, j * G + g, e * C:(e + 1) * C])
                    ins.then_inc(S["heads_made"], 1)
                for u in MLP.get(t, []):
                    mlp_unit(0, u)
                n = t - AT - 3
                if 0 <= n < N:
                    wait(pe, "hid_normed", n + 1)
                    wait(pe, "queries_ready", 2 * G)
                    wait(pe, "values_ready", 4 * 4)
                    wait(pe, "hidf_ready", 2 * n)
                    for g in range(G):
                        ins = pe.transpose(psum[:, FILL, g * P:(g + 1) * P], hn[:, n % 2, g * P:(g + 1) * P], ident[:])
                    ins.then_inc(S["hid_turned"], 1)
                for u in MLP.get(t + 0.3, []):
                    mlp_unit(0, u)
                n = t - AT
                if 0 <= n < N:
                    if n == 0:
                        wait(pe, "relu_in", N)
                    wait(pe, "probs_ready", n + 1)
                    wait(pe, "probst_ready", 2 * n)
                    for i in range(HP):
                        ins = pe.transpose(probsT_ps[:, i, :], probs[:, n % 2, i * P:(i + 1) * P], ident[:])
                    ins.then_inc(S["probs_turned"], 1)
                if t == AT:
                    make_queries(1, 1)
                n = t - AT - 1
                if 0 <= n < N:
                    if n == 0:
                        pe.wait_ge(w_loaded["c"], 16)
                    wait(pe, "heads_ready", 2 * (n + 1))
                    for c in range(G):
                        ins = mm(halfbank(HEADS, 0), hdT[:, c, :], wc[:, c, :], c == 0, c == G - 1)
                    ins.then_inc(S["attn_made"], 1)
                for u in MLP.get(t + 0.6, []):
                    mlp_unit(0, u)
            for m in range(M):
                mlp_unit(1, ("fc", m))
            for i in range(NH):
                mlp_unit(1, ("pj", i))


_OUT = ((16, 64, 256), "float32")


def kernel(**inputs):
    import numpy as _np
    import concourse.bacc as _bacc
    from concourse import mybir as _mybir
    from concourse.bass_utils import run_bass_kernel_spmd as _run

    nc = _bacc.Bacc("TRN2", target_bir_lowering=False, num_devices=1)
    arrays, aps = {}, {}
    for name, a in inputs.items():
        a = _np.ascontiguousarray(a)
        if a.dtype == _np.bool_:
            a = a.view(_np.uint8)
        arrays[f"in_{name}_dram"] = a
        aps[name] = nc.dram_tensor(f"in_{name}_dram", a.shape, _mybir.dt.from_np(a.dtype), kind="ExternalInput").ap()
    out = nc.dram_tensor("out_0_dram", _OUT[0], _mybir.dt.from_np(_np.dtype(_OUT[1])), kind="ExternalOutput").ap()
    xattn_two_layers(nc, aps, out)
    r = _run(nc, [arrays], core_ids=[0])
    return r.results[0]["out_0_dram"]
```
